# Optimizing a Trainium2 kernel written in Bass

```python
import numpy as np
import jax
import jax.numpy as jnp

def _softmax(x, axis=-1):
    return jax.nn.softmax(x, axis=axis)

def _gelu(x):
    return jax.nn.gelu(x, approximate=True)

def _silu(x):
    return jax.nn.silu(x)

def _sigmoid(x):
    return jax.nn.sigmoid(x)

def _layernorm(x, axis=-1, eps=1e-05):
    m = jnp.mean(x, axis=axis, keepdims=True)
    v = jnp.var(x, axis=axis, keepdims=True)
    return (x - m) / jnp.sqrt(v + eps)

def _scatter_add(tgt, idx, src, axis=0):
    return tgt.at[idx].add(src)

def _segment_sum(src, seg, n):
    return jax.ops.segment_sum(src, seg, n)
kernel_name = 'mk_flamingo_gated_d1_seqx_r2_745614'

def setup_inputs(seed: int=0):
    np.random.seed(seed)
    _w = jnp.asarray

    def _rec_inputs():
        import jax
        import jax.numpy as jnp
        _rk = jax.random.key(seed)
        x = -0.0002928 + 1 * jax.random.normal(jax.random.fold_in(_rk, 1), (2, 2048, 512), jnp.float32)
        _lenS = 2048 - jax.random.randint(jax.random.fold_in(_rk, 7), (2,), 0, max(1, 2048 // 4) + 1, jnp.int32)
        _lenS2 = 128 - jax.random.randint(jax.random.fold_in(_rk, 8), (2,), 0, max(1, 128 // 4) + 1, jnp.int32)
        _ctx_1024P = jax.random.normal(jax.random.fold_in(_rk, 11), (2, 16, 512), jnp.float32)
        _ctx_1024c = jax.random.dirichlet(jax.random.fold_in(_rk, 511), 0.3 * jnp.ones((16,), jnp.float32), (2, 128))
        _ctx_1024t = jnp.einsum('bsk,bkd->bsd', _ctx_1024c, _ctx_1024P)
        _ctx_1024t = _ctx_1024t * jax.lax.rsqrt(jnp.mean(jnp.square(_ctx_1024t)) + 1e-12) * 0.953939
        ctx_1024 = -1.39393e-06 + 0.999914 * (_ctx_1024t + 0.3 * jax.random.normal(jax.random.fold_in(_rk, 611), (2, 128, 512), jnp.float32))
        _validS = jnp.arange(2048)[None, :] < _lenS[:, None]
        _validS2 = jnp.arange(128)[None, :] < _lenS2[:, None]
        _causal = jnp.tril(jnp.ones((2048, 2048), dtype=bool))
        mask_Bx1x1xS2_ik0 = jnp.where(jnp.broadcast_to(_validS2[:, None, None, :], (2, 1, 1, 128)), 0, 1).astype(jnp.int32)
        mask_1x1xSxS2_ik0 = jnp.where(jnp.broadcast_to(_validS2[0:1, None, None, :], (1, 1, 2048, 128)), 0, 1).astype(jnp.int32)
        _g = jax.random.normal(jax.random.fold_in(_rk, 9001), (2, 1), jnp.float32)
        _g = jnp.sign(_g) * jnp.maximum(jnp.abs(_g), 1.0) + (_g == 0) * 1.0
        g_xattn = _g[0]
        g_ffn = _g[1]
        return (x, ctx_1024, mask_Bx1x1xS2_ik0, mask_1x1xSxS2_ik0, g_xattn, g_ffn)
    x, ctx_1024, mask_Bx1x1xS2_ik0, mask_1x1xSxS2_ik0, g_xattn, g_ffn = _rec_inputs()

    def _L0_xattn_setup():
        import jax, jax.numpy as jnp
        import numpy as np
        E, H = (512, 16)
        N, S, T = (2, 1024, 1024)
        key = jax.random.key(seed)
        ks = jax.random.split(key, 8)
        scale = 1.0 / np.sqrt(E)
        q = jax.random.normal(ks[0], (N, S, E), dtype=jnp.float32)
        k = jax.random.normal(ks[1], (N, T, E), dtype=jnp.float32)
        v = jax.random.normal(ks[2], (N, T, E), dtype=jnp.float32)
        pad_mask = jax.random.randint(ks[3], (N, 1, 1, T), 0, 2, dtype=jnp.int32)
        subsq_mask = jnp.tril(jnp.ones((S, T), dtype=jnp.int32))[None, None]
        Wq = jax.random.normal(ks[4], (E, E), dtype=jnp.float32) * scale
        Wk = jax.random.normal(ks[5], (E, E), dtype=jnp.float32) * scale
        Wv = jax.random.normal(ks[6], (E, E), dtype=jnp.float32) * scale
        bq = jnp.zeros((E,), dtype=jnp.float32)
        bk = jnp.zeros((E,), dtype=jnp.float32)
        bv = jnp.zeros((E,), dtype=jnp.float32)
        return {'query': q, 'key': k, 'value': v, 'pad_mask': pad_mask, 'subsq_mask': subsq_mask, 'Wq': Wq, 'bq': bq, 'Wk': Wk, 'bk': bk, 'Wv': Wv, 'bv': bv}
    _L0_xattn_all = _L0_xattn_setup()
    _L0_xattn_in = {k: v for k, v in _L0_xattn_all.items() if k in ('Wq', 'bq', 'Wk', 'bk', 'Wv', 'bv')}
    del _L0_xattn_all

    def _L0_ffn_setup():
        import jax, jax.numpy as jnp
        import numpy as np
        TOP_K = 2
        NUM_EXPERTS = 8
        key = jax.random.key(seed)
        ks = jax.random.split(key, 8)
        h, d, ds, E = (512, 256, 512, NUM_EXPERTS)
        s = 1.0 / np.sqrt(h)
        return {'x': jax.random.normal(ks[0], (2, 1024, h), jnp.float32), 'router': jax.random.normal(ks[1], (h, E), jnp.float32) * s, 'experts_gate': jax.random.normal(ks[2], (E, h, d), jnp.float32) * s, 'experts_up': jax.random.normal(ks[3], (E, h, d), jnp.float32) * s, 'experts_down': jax.random.normal(ks[4], (E, d, h), jnp.float32) * (1.0 / np.sqrt(d)), 'shared_gate': jax.random.normal(ks[5], (h, ds), jnp.float32) * s, 'shared_up': jax.random.normal(ks[6], (h, ds), jnp.float32) * s, 'shared_down': jax.random.normal(ks[7], (ds, h), jnp.float32) * (1.0 / np.sqrt(ds))}
    _L0_ffn_all = _L0_ffn_setup()
    _L0_ffn_in = {k: v for k, v in _L0_ffn_all.items() if k in ('router', 'experts_gate', 'experts_up', 'experts_down', 'shared_gate', 'shared_up', 'shared_down')}
    del _L0_ffn_all
    return {'x': x, 'ctx_1024': ctx_1024, 'mask_Bx1x1xS2_ik0': mask_Bx1x1xS2_ik0, 'mask_1x1xSxS2_ik0': mask_1x1xSxS2_ik0, 'g_xattn': g_xattn, 'g_ffn': g_ffn, 'L0_xattn_Wq': _L0_xattn_in['Wq'], 'L0_xattn_bq': _L0_xattn_in['bq'], 'L0_xattn_Wk': _L0_xattn_in['Wk'], 'L0_xattn_bk': _L0_xattn_in['bk'], 'L0_xattn_Wv': _L0_xattn_in['Wv'], 'L0_xattn_bv': _L0_xattn_in['bv'], 'L0_ffn_router': _L0_ffn_in['router'], 'L0_ffn_experts_gate': _L0_ffn_in['experts_gate'], 'L0_ffn_experts_up': _L0_ffn_in['experts_up'], 'L0_ffn_experts_down': _L0_ffn_in['experts_down'], 'L0_ffn_shared_gate': _L0_ffn_in['shared_gate'], 'L0_ffn_shared_up': _L0_ffn_in['shared_up'], 'L0_ffn_shared_down': _L0_ffn_in['shared_down']}

def reference(x, ctx_1024, mask_Bx1x1xS2_ik0, mask_1x1xSxS2_ik0, g_xattn, g_ffn, L0_xattn_Wq, L0_xattn_bq, L0_xattn_Wk, L0_xattn_bk, L0_xattn_Wv, L0_xattn_bv, L0_ffn_router, L0_ffn_experts_gate, L0_ffn_experts_up, L0_ffn_experts_down, L0_ffn_shared_gate, L0_ffn_shared_up, L0_ffn_shared_down):
    import jax
    import jax.numpy as jnp

    def _L0_xattn_ref(query, key, value, pad_mask, subsq_mask, Wq, bq, Wk, bk, Wv, bv):
        import jax, jax.numpy as jnp
        import numpy as np
        E, H = (512, 16)
        N, S, T = (2, 1024, 1024)
        n, s, e = query.shape
        t = value.shape[1]
        d = e // H
        q = (query @ Wq.T + bq).reshape(n, s, H, d).transpose(0, 2, 1, 3)
        k = (key @ Wk.T + bk).reshape(n, t, H, d).transpose(0, 2, 1, 3)
        v = (value @ Wv.T + bv).reshape(n, t, H, d).transpose(0, 2, 1, 3)
        att = jnp.einsum('bhsd,bhtd->bhst', q, k) / jnp.sqrt(jnp.float32(d))
        att = jnp.where(pad_mask == 0, jnp.float32(-1000000000.0), att)
        att = jnp.where(subsq_mask == 0, jnp.float32(-1000000000.0), att)
        prob = jax.nn.softmax(att, axis=-1)
        out = jnp.einsum('bhst,bhtd->bhsd', prob, v)
        return out.transpose(0, 2, 1, 3).reshape(n, s, e)

    def _L0_ffn_ref(x, router, experts_gate, experts_up, experts_down, shared_gate, shared_up, shared_down):
        import jax, jax.numpy as jnp
        import numpy as np
        TOP_K = 2
        NUM_EXPERTS = 8
        b, s, h = x.shape
        E = router.shape[1]
        shared_act = jax.nn.silu(jnp.einsum('bsh,hd->bsd', x, shared_gate))
        shared_up_out = jnp.einsum('bsh,hd->bsd', x, shared_up)
        shared_out = jnp.einsum('bsd,dh->bsh', shared_act * shared_up_out, shared_down)
        router_probs = jax.nn.softmax(jnp.einsum('bsh,he->bse', x, router), axis=-1)
        topk_probs, topk_idx = jax.lax.top_k(router_probs, TOP_K)
        coef = jnp.sum(jax.nn.one_hot(topk_idx, E, dtype=x.dtype) * topk_probs[..., None], axis=2)
        coef = coef.reshape(b * s, E)
        x_flat = x.reshape(b * s, h)
        gate = jnp.einsum('th,ehd->etd', x_flat, experts_gate)
        up = jnp.einsum('th,ehd->etd', x_flat, experts_up)
        expert_out = jnp.einsum('etd,edh->eth', jax.nn.silu(gate) * up, experts_down)
        routed = jnp.einsum('eth,te->th', expert_out, coef)
        return routed.reshape(b, s, h) + shared_out
    x = x + jnp.tanh(g_xattn[0]) * _L0_xattn_ref(_layernorm(x, axis=-1), ctx_1024, ctx_1024, mask_Bx1x1xS2_ik0, mask_1x1xSxS2_ik0, L0_xattn_Wq, L0_xattn_bq, L0_xattn_Wk, L0_xattn_bk, L0_xattn_Wv, L0_xattn_bv)
    x = x + jnp.tanh(g_ffn[0]) * _L0_ffn_ref(_layernorm(x, axis=-1), L0_ffn_router, L0_ffn_experts_gate, L0_ffn_experts_up, L0_ffn_experts_down, L0_ffn_shared_gate, L0_ffn_shared_up, L0_ffn_shared_down)
    return x

_drawn_inputs = setup_inputs


def setup_inputs(seed=0):
    import zlib

    import numpy as np

    out = dict(_drawn_inputs(seed))
    spreads = {'L0_xattn_bq': (0.0, 0.1), 'L0_xattn_bk': (0.0, 0.1), 'L0_xattn_bv': (0.0, 0.1)}
    factors = {}
    for name, (base, spread) in spreads.items():
        noise = np.random.default_rng([zlib.crc32(name.encode()), seed]).standard_normal(out[name].shape)
        drawn = base * np.exp(spread * noise) if base else spread * noise
        out[name] = jnp.asarray(drawn.astype(out[name].dtype))
    for name, factor in factors.items():
        out[name] = (out[name] * factor).astype(out[name].dtype)
    return out
```

```python
from contextlib import ExitStack

import concourse.bass as bass
import numpy as np
from concourse import mybir

F32, F16 = mybir.dt.float32, mybir.dt.float16
I32, U32 = mybir.dt.int32, mybir.dt.uint32
ALU = mybir.AluOpType
ACT = mybir.ActivationFunctionType
AX = mybir.AxisListType
RMAX = bass.bass_isa.ReduceOp.max

P = 128
B, S, E = 2, 2048, 512
T = 128
H, D = 16, 32
NX, DX, DS, TOP = 8, 256, 512, 2
TOK = B * S
NT = TOK // P
EC = E // P
HG = H // EC
REGION = TOK
SLOTS = TOK * TOP // P + NX
LISTS = (NX + 1) * REGION
EPS = 1e-5
MASKED = -1e30
LOWEST = -3e38
X_SCALE = 1024.0
W_TOP = 16384.0
TINY = 2.0 ** -100
EXPONENT = 0x7F800000


def build(nc, x, ctx_t, pad, sub, gates, wq_t, wk_t, wv_t, bq, bk, bv, router, w_gu, w_down, s_gu, s_down, out):
    x_tiles = x.rearrange("b (j p) d -> (b j) p d", p=P)
    out_tiles = out.rearrange("b (j p) d -> (b j) p d", p=P)
    sub_tiles = sub.rearrange("a b (j p) t -> (a b j) p t", p=P)
    HALF = NT // B

    x1_dram = nc.dram_tensor("x1_rows", [TOK, E], F32).ap()
    xn_dram = nc.dram_tensor("normed_rows", [TOK, E], F32).ap()
    list_dram = nc.dram_tensor("token_of_row", [LISTS, 1], I32).ap()
    y_dram = nc.dram_tensor("expert_rows", [SLOTS * P, E], F32).ap()

    with ExitStack() as ctx:
        def sb(name, shape, dt=F32):
            return ctx.enter_context(nc.sbuf_tensor(name, shape, dt))

        def sems(names):
            return [ctx.enter_context(nc.semaphore(n)) for n in names.split()]

        bank = [ctx.enter_context(nc.psum_tensor(f"bank{i}", [P, 512], F32)) for i in range(8)]

        GU = NX * EC * 2 * DX
        SGU = EC * 2 * DS
        gu = sb("gu", [P, 2, GU], F16)
        sgu = sb("sgu", [P, 2, SGU], F16)
        wd = sb("wd", [P, NX * (DX // P) * E])
        gu_raw = gu[:, :, :].rearrange("p a n -> p (a n)").bitcast(F32)
        sgu_raw = sgu[:, :, :].rearrange("p a n -> p (a n)").bitcast(F32)

        ident = sb("ident", [P, P])
        before = sb("before", [P, P], F16)
        ones = sb("ones", [P, P], F16)
        pad_raw = sb("pad_raw", [P, B, T], I32)
        pad_bias = sb("pad_bias", [P, B, T])
        pad_keep = sb("pad_keep", [P, B, T])
        gate_raw = sb("gate_raw", [P, 2])
        gate = sb("gate", [P, 2])
        bq_s = sb("bq_s", [P, EC])
        bk_s = sb("bk_s", [P, EC])
        router_s = sb("router_s", [P, EC, NX])
        half_power = sb("half_power", [P, 1])
        peak = sb("peak", [P, 16])
        peak_all = sb("peak_all", [P, 2])
        w_scale = sb("w_scale", [P, 2])
        w_back = sb("w_back", [P, 2])
        expert_no = sb("expert_no", [P, NX])
        region_at = sb("region_at", [P, NX])
        token_no = sb("token_no", [P, HALF, B], I32)
        zeros_i = sb("zeros_i", [P, LISTS // P], I32)
        seen = sb("seen", [P, NX], F16)
        prob_all = sb("prob_all", [P, NT * TOP])
        row_list = sb("row_list", [P, NT * TOP])
        row_all = sb("row_all", [P, NT * TOP], U32)
        slot_row = sb("slot_row", [P, SLOTS], I32)
        slot_expert = sb("slot_expert", [P, SLOTS], I32)

        ARENA = 21 * 1024
        arena = sb("arena", [P, ARENA])
        top = [0]

        def carve(cols):
            top[0] += cols
            assert top[0] <= ARENA, top[0]
            return arena[:, top[0] - cols:top[0]]

        wq = carve(EC * E).bitcast(F16).rearrange("p (a n) -> p a n", a=2)
        kbd = carve(B * EC * HG * T).rearrange("p (b c n) -> p b c n", b=B, c=EC)
        vaug = carve(B * H * (D + 1)).rearrange("p (b h d) -> p b h d", b=B, h=H)
        score = [carve(H * T) for _ in range(2)]
        wk_s = score[0].rearrange("p (c n) -> p c n", c=EC)
        wv_s = score[1].rearrange("p (c n) -> p c n", c=EC)
        probs_t = [carve(HG * T) for _ in range(2)]
        x_in = [carve(E) for _ in range(2)]
        x_res = [carve(E) for _ in range(2)]
        wq_raw = arena[:, top[0] - 4 * E:top[0]]
        xn = [carve(E) for _ in range(2)]
        x_hi, x_lo = carve(E // 2).bitcast(F16), carve(E // 2).bitcast(F16)
        q_t = [carve(E) for _ in range(2)]
        attn = carve(E)
        x1 = [carve(E) for _ in range(2)]
        xn2 = [carve(E) for _ in range(2)]
        xn2_t = carve(E)
        bv_s = attn
        ctx_s = arena[:, top[0] - 3 * E:top[0] - E].rearrange("p (c n) -> p c n", c=EC)
        sub_raw = carve(T).bitcast(I32)
        sub_bias = carve(T)
        mask_bias = [carve(T) for _ in range(2)]
        peaks_of = [carve(H) for _ in range(2)]
        peaks_neg = carve(HG)
        stats = [carve(6) for _ in range(2)]
        stats2 = [carve(6) for _ in range(2)]
        mv, mv2 = [carve(2) for _ in range(2)], [carve(2) for _ in range(2)]
        norm, norm2 = [carve(3) for _ in range(2)], [carve(3) for _ in range(2)]
        inv_sum = carve(H)
        logit_top, logit_neg = carve(NX), carve(1)
        r_exp, r_sum, r_inv, r_prob, r_top = carve(NX), carve(1), carve(1), carve(NX), carve(NX)
        r_idx = carve(NX).bitcast(U32)
        r_idxf = carve(TOP)
        first = [carve(NX) for _ in range(2)]
        second = [carve(NX) for _ in range(2)]
        chosen = [carve(NX // 2).bitcast(F16) for _ in range(2)]
        at_row = carve(NX)
        junk = [carve(NX) for _ in range(2)]
        row_f = carve(TOP)
        row_i = [carve(TOP).bitcast(U32) for _ in range(2)]
        tok_i = [carve(1).bitcast(I32) for _ in range(2)]

        top[0] = 0
        id_in = [carve(1).bitcast(I32) for _ in range(4)]
        xg = [carve(E) for _ in range(4)]
        g_hi = [carve(E // 2).bitcast(F16) for _ in range(2)]
        g_lo = [carve(E // 2).bitcast(F16) for _ in range(2)]
        g_act = [carve(DX) for _ in range(2)]
        g_h = [carve(DX) for _ in range(2)]
        g_ht = carve(DX)
        g_y = [carve(E) for _ in range(2)]
        reached = carve(NX * NT)
        n_tiles, upto = carve(NX), carve(NX)
        below = carve(NX * NX)
        step_at, slot_no = carve(NT), carve(SLOTS)
        passed = carve(SLOTS * NX)
        passed_n = carve(SLOTS * NX)
        expert_f, base_f, row_sf = carve(SLOTS), carve(SLOTS), carve(SLOTS)
        later = carve(NT * TOP * (NX - 1))
        moved, row_slots = carve(NX - 1), carve(NT * TOP)

        top[0] = 0
        f_x = [carve(E) for _ in range(2)]
        f_x1 = [carve(E) for _ in range(2)]
        f_idx = [[carve(1).bitcast(U32) for _ in range(TOP)] for _ in range(2)]
        f_y = [[carve(E) for _ in range(TOP)] for _ in range(2)]
        f_hi = [carve(E // 2).bitcast(F16) for _ in range(2)]
        f_lo = [carve(E // 2).bitcast(F16) for _ in range(2)]
        f_act = [carve(DS) for _ in range(2)]
        f_h = [carve(DS) for _ in range(2)]
        f_ht = carve(DS)
        f_c1, f_c2 = carve(E), carve(E)
        f_out = [carve(E) for _ in range(2)]
        swd = arena[:, ARENA - DS // P * E:].rearrange("p (c n) -> p c n", c=DS // P)

        small_in, kv_in, wq_in, raw_in, down_in, swd_in = sems("small_in kv_in wq_in raw_in down_in swd_in")
        chunk_in = sems("chunk_in0 chunk_in1 chunk_in2 chunk_in3")
        x_here, res_here, xn2_out, x1_out, rows_out = (sems(f"{n}0 {n}1") for n in ("x_here", "res_here", "xn2_out", "x1_out", "rows_out"))
        sub_here, list_zero = sems("sub_here list_zero")
        id_here, xg_here = (sems(f"{n}0 {n}1 {n}2 {n}3") for n in ("id_here", "xg_here"))
        y_out = sems("y_out0 y_out1")
        f_x_here, f_x1_here, f_y_here, f_out_done = (sems(f"{n}0 {n}1") for n in ("f_x_here", "f_x1_here", "f_y_here", "f_out_done"))
        dve_passed, pool_passed, peak_step = sems("dve_passed pool_passed peak_step")
        const_set, pool_set, peak_set, scale_set, prep_hi, prep_lo, kv_mm, kv_set, gate_set = sems(
            "const_set pool_set peak_set scale_set prep_hi prep_lo kv_mm kv_set gate_set")
        ln1_stats, ln1_mv, ln1_eps, ln1_std, ln1_norm, xn_ready = sems("ln1_stats ln1_mv ln1_eps ln1_std ln1_norm xn_ready")
        xt_done, hi_ready, lo_ready, q_done, q_ready = sems("xt_done hi_ready lo_ready q_done q_ready")
        sub_set, mask_half, mask_set = sems("sub_set mask_half mask_set")
        s_done, max_done, shift_done, exp_done, pt_done, pt_ready, av_done, neg_done = sems(
            "s_done max_done shift_done exp_done pt_done pt_ready av_done neg_done")
        inv_done, attn_done = sems("inv_done0 inv_done1"), sems("attn_done0 attn_done1")
        x1_ready, ln2_stats, ln2_mv, ln2_eps, ln2_std, xn2_ready = sems(
            "x1_ready ln2_stats ln2_mv ln2_eps ln2_std xn2_ready")
        x2t_done, x2t_ready, logits_done, logit_shift, r_exp_done, r_inv_done, r_top_done = sems(
            "x2t_done x2t_ready logits_done logit_shift r_exp_done r_inv_done r_top_done")
        r_idx_done, first_done, chosen_done, rank_done, at_row_done, row_f_done, row_ready, tok_ready, seen_done, seen_zero = sems(
            "r_idx_done first_done chosen_done rank_done at_row_done row_f_done row_ready tok_ready seen_done seen_zero")
        pass1_over, pass2_over, counts_done, scale_step, plan_step, plan_iota, plan_ready = sems(
            "pass1_over pass2_over counts_done scale_step plan_step plan_iota plan_ready")
        gt_done, g_hi_ready, g_lo_ready, gu_done, g_act_ready, g_h_ready, g_ht_done, g_ht_ready, gd_done, g_y_ready = sems(
            "gt_done g_hi_ready g_lo_ready gu_done g_act_ready g_h_ready g_ht_done g_ht_ready gd_done g_y_ready")
        f_idx_ready, ft_done, f_hi_ready, f_lo_ready, fu_done, f_act_ready, f_h_ready, f_ht_done, f_ht_ready, fd_done, f_c1_done, f_c2_done, f_out_ready = sems(
            "f_idx_ready ft_done f_hi_ready f_lo_ready fu_done f_act_ready f_h_ready f_ht_done f_ht_ready fd_done f_c1_done f_c2_done f_out_ready")

        def tile(J, v, lag, deep=2, span=2):
            return span * J + (v - lag), span // deep * J + (v - lag) // deep, (v - lag) % deep

        def live(n, total):
            return not isinstance(n, int) or 0 <= n < total

        def need(eng, sem, value):
            if not isinstance(value, int) or value > 0:
                eng.wait_ge(sem, value)

        def hold(eng, passed_by, *waits):
            for sem, value in waits:
                need(eng, sem, value)
            if not all(isinstance(value, int) for _, value in waits):
                eng.sem_inc(passed_by, 1)

        def pipeline(eng, body, total, lag, span=2, beside=None):
            head = (lag + 2 + span - 1) // span

            def written_out(its):
                for it in its:
                    body(it // span, it % span)
                    if beside is not None:
                        beside(it)

            written_out(range(head * span))
            with eng.Fori(head, total // span) as J:
                for v in range(span):
                    body(J, v)
            written_out(range(total, total + lag))

        def group(n, k, of=EC):
            return n * of + k + 1

        RANK_AT = 64

        LAG1, LAG2, LAG3, SPAN2 = 8, 3, 3, 4
        HEAD1 = (LAG1 + 3) // 2 * 2
        CH = 2048
        chunks = [(gu_raw, gu, i * CH) for i in range(GU // CH)] + [(sgu_raw, sgu, i * CH) for i in range(SGU // CH)]
        gu_flat = gu[:, :, :].rearrange("p a n -> p (a n)")
        w_gu_flat = w_gu.rearrange("p x c n -> p (x c n)")
        s_gu_flat = s_gu.rearrange("p c n -> p (c n)")

        STAGES = NX * (DX // P) * E // CH
        stage = [wd[:, i * CH:(i + 1) * CH] for i in range(STAGES)]
        per_tail = -(-len(chunks) // LAG1)

        def chunk_src(i):
            n = GU // CH
            return w_gu_flat[:, i * CH:(i + 1) * CH] if i < n else s_gu_flat[:, (i - n) * CH:(i - n + 1) * CH]

        block = ctx.enter_context(nc.Block())

        @block.sync
        def _(sp):
            for dst, src in ((gate_raw[:, :], gates), (bq_s[:, :], bq), (bk_s[:, :], bk), (bv_s, bv),
                             (router_s[:, :, :], router), (pad_raw[:, :, :], pad)):
                sp.dma_start(dst, src).then_inc(small_in, 16)
            for dst, src in ((ctx_s, ctx_t), (wk_s, wk_t), (wv_s, wv_t)):
                sp.dma_start(dst, src).then_inc(kv_in, 16)
            sp.dma_start(wq_raw, wq_t.rearrange("p c n -> p (c n)")).then_inc(wq_in, 16)
            sp.wait_ge(prep_lo, 1)

            def body(J, v):
                n, j, u = tile(J, v, 6)
                if live(n, NT):
                    sp.wait_ge(x1_ready, n + 1)
                    sp.dma_start(x1_dram[bass.ds(j * P + u * S, P), :], x1[u]).then_inc(x1_out[u], 16)
                n, j, u = tile(J, v, 7)
                if live(n, NT):
                    sp.wait_ge(xn2_ready, n + 1)
                    sp.dma_start(xn_dram[bass.ds(j * P + u * S, P), :], xn2[u]).then_inc(xn2_out[u], 16)
                n, j, u = tile(J, v, 0)
                if live(n, NT):
                    need(sp, xn_ready, n - 1)
                    sp.dma_start(x_in[u], x_tiles[bass.ds(j + u * HALF, 1)].rearrange("a p d -> (a p) d")).then_inc(x_here[u], 16)
                    if u == 0:
                        need(sp, sub_set, j)
                        sp.dma_start(sub_raw, sub_tiles[bass.ds(j, 1)].rearrange("a p d -> (a p) d")).then_inc(sub_here, 16)
                n, j, u = tile(J, v, 4)
                if live(n, NT):
                    need(sp, x1_ready, n - 1)
                    sp.dma_start(x_res[u], x_tiles[bass.ds(j + u * HALF, 1)].rearrange("a p d -> (a p) d")).then_inc(res_here[u], 16)

            def beside(it):
                if it < NT:
                    return
                for i in range((it - NT) * per_tail + STAGES, min((it - NT + 1) * per_tail + STAGES, len(chunks))):
                    sp.wait_ge(prep_lo, i - STAGES + 2)
                    sp.dma_start(stage[i % STAGES], chunk_src(i)).then_inc(chunk_in[i % STAGES], 16)

            pipeline(sp, body, NT, LAG1, beside=beside)
            sp.wait_ge(prep_lo, 1 + len(chunks))
            sp.dma_start(wd[:, :], w_down.rearrange("p x c n -> p (x c n)")).then_inc(down_in, 16)
            for u in range(2):
                sp.wait_ge(x1_out[u], 16 * HALF)
                sp.wait_ge(xn2_out[u], 16 * HALF)
                sp.wait_ge(rows_out[u], 16 * TOP * HALF)
            sp.wait_ge(plan_ready, 2)
            sp.drain().then_inc(pass1_over, 1)
            sp.wait_ge(pass1_over, 5)
            sp.dma_start(swd, s_down).then_inc(swd_in, 16)

            def body2(J, v):
                s, j, u = tile(J, v, 0, 4, SPAN2)
                if live(s, SLOTS):
                    need(sp, xg_here[u], 16 * j)
                    r = sp.value_load(slot_row[0:1, bass.ds(s, 1)], min_val=0, max_val=LISTS - P)
                    sp.dma_start(id_in[u], list_dram[bass.ds(r, P), :]).then_inc(id_here[u], 16)

            pipeline(sp, body2, SLOTS, LAG2, SPAN2)
            sp.drain().then_inc(pass2_over, 1)
            sp.wait_ge(pass2_over, 5)

            def body3(J, v):
                n, j, u = tile(J, v, 0)
                if live(n, NT):
                    need(sp, ft_done, n - 1)
                    sp.dma_start(f_x[u], xn_dram[bass.ds(j * P + u * S, P), :]).then_inc(f_x_here[u], 16)
                n, j, u = tile(J, v, 1)
                if live(n, NT):
                    need(sp, f_out_ready, n - 1)
                    sp.dma_start(f_x1[u], x1_dram[bass.ds(j * P + u * S, P), :]).then_inc(f_x1_here[u], 16)

            pipeline(sp, body3, NT, LAG3)

        @block.gpsimd
        def _(pool):
            g = nc.gpsimd
            g.memset(ident[:, :], 0.0).then_inc(pool_set, 1)
            g.memset(ones[:, :], 1.0).then_inc(pool_set, 1)
            g.memset(half_power[:, :], -0.5).then_inc(pool_set, 1)
            g.memset(zeros_i[:, :], 0).then_inc(pool_set, 1)
            g.memset(seen[:, :], 0.0).then_inc(seen_zero, 1)
            pool.wait_ge(pool_set, 4)
            pool.dma_start(list_dram.rearrange("(p n) a -> p (n a)", p=P), zeros_i[:, :]).then_inc(list_zero, 16)
            g.affine_select(out=ident[:, :], in_=ident[:, :], compare_op=ALU.not_equal, fill=1.0, base=0,
                            pattern=[[-1, P]], channel_multiplier=1).then_inc(const_set, 1)
            g.affine_select(out=before[:, :], in_=ones[:, :], compare_op=ALU.is_gt, fill=0.0, base=0,
                            pattern=[[1, P]], channel_multiplier=-1).then_inc(const_set, 1)
            g.iota(expert_no[:, :], [[1, NX]], base=0, channel_multiplier=0, allow_small_or_imprecise_dtypes=True).then_inc(const_set, 1)
            g.iota(region_at[:, :], [[REGION, NX]], base=0, channel_multiplier=0, allow_small_or_imprecise_dtypes=True).then_inc(const_set, 1)
            g.iota(token_no[:, :, :], [[P, HALF], [S, B]], base=0, channel_multiplier=1).then_inc(const_set, 1)
            pool.wait_ge(small_in, 96)
            g.tensor_scalar(pad_bias[:, :, :], pad_raw[:, :, :], 0.0, MASKED, ALU.is_equal, ALU.mult).then_inc(const_set, 1)
            pool.wait_ge(const_set, 6)
            g.tensor_scalar(pad_keep[:, :, :], pad_bias[:, :, :], 0.0, None, ALU.is_equal).then_inc(const_set, 1)
            pool.wait_ge(peak_set, 1)
            g.partition_all_reduce(peak_all[:, 0:1], peak[:, 0:1], P, RMAX).then_inc(scale_set, 1)
            pool.wait_ge(const_set, 7)
            pool.wait_ge(list_zero, 16)

            def body(J, v):
                def shift(k):
                    n, j, u = tile(J, v, 3)
                    if live(n, NT):
                        pool.wait_ge(max_done, group(n, k))
                        sc = score[u].rearrange("p (h t) -> p h t", h=H)[:, k * HG:(k + 1) * HG, :]
                        mx = peaks_of[u][:, k * HG:(k + 1) * HG].unsqueeze(2).to_broadcast([P, HG, T])
                        g.tensor_tensor(sc, sc, mx, ALU.subtract).then_inc(shift_done, 1)

                shift(0)
                n, j, u = tile(J, v, 2)
                if live(n, NT):
                    if u == 0:
                        hold(pool, pool_passed, (sub_here, 16 * (j + 1)))
                        g.tensor_scalar(sub_bias, sub_raw, 0.0, MASKED, ALU.is_equal, ALU.mult).then_inc(sub_set, 1)
                    pool.wait_ge(sub_set, j + 1)
                    need(pool, max_done, group(n - 2, EC - 1))
                    g.tensor_tensor(mask_bias[u], sub_bias, pad_keep[:, u, :], ALU.mult).then_inc(mask_half, 1)
                shift(1)
                if live(n, NT):
                    pool.wait_ge(mask_half, n + 1)
                    g.tensor_tensor(mask_bias[u], mask_bias[u], pad_bias[:, u, :], ALU.add).then_inc(mask_set, 1)
                shift(2)
                n, j, u = tile(J, v, 5)
                if live(n, NT):
                    hold(pool, pool_passed, (ln2_mv, n + 1))
                    g.tensor_scalar(norm2[u][:, 0:1], mv2[u][:, 1:2], EPS, None, ALU.add).then_inc(ln2_eps, 1)
                    pool.wait_ge(ln2_eps, n + 1)
                    g.tensor_tensor(norm2[u][:, 1:2], norm2[u][:, 0:1], half_power[:, :], ALU.pow).then_inc(ln2_std, 1)
                n, j, u = tile(J, v, 0)
                if live(n, NT):
                    hold(pool, pool_passed, (ln1_mv, n + 1))
                    g.tensor_scalar(norm[u][:, 0:1], mv[u][:, 1:2], EPS, None, ALU.add).then_inc(ln1_eps, 1)
                    pool.wait_ge(ln1_eps, n + 1)
                    g.tensor_tensor(norm[u][:, 1:2], norm[u][:, 0:1], half_power[:, :], ALU.pow).then_inc(ln1_std, 1)
                    hold(pool, pool_passed, (ln1_std, n + 1))
                    g.tensor_scalar(norm[u][:, 2:3], mv[u][:, 0:1], norm[u][:, 1:2], -1.0, ALU.mult, ALU.mult).then_inc(ln1_norm, 1)
                n, j, u = tile(J, v, 8)
                if live(n, NT):
                    need(pool, rows_out[u], 16 * TOP * j)
                    g.tensor_copy(tok_i[u], token_no[:, :, :].rearrange("p j b -> p (j b)")[:, bass.ds(n, 1)]).then_inc(tok_ready, 1)
                    hold(pool, pool_passed, (tok_ready, n + 1), (row_ready, n + 1))
                    for k in range(TOP):
                        g.indirect_dma_start(list_dram, bass.IndirectOffsetOnAxis(ap=row_i[u][:, k:k + 1], axis=0),
                                             tok_i[u], None).then_inc(rows_out[u], 16)

            def beside(it):
                if it == HEAD1 - 1:
                    pool.wait_ge(peak_set, 2)
                    g.partition_all_reduce(peak_all[:, 1:2], peak[:, 15:16], P, RMAX).then_inc(scale_set, 1)

            pipeline(pool, body, NT, LAG1, beside=beside)
            g.drain().then_inc(pass1_over, 1)
            pool.wait_ge(pass1_over, 4)
            g.iota(step_at, [[P, NT]], base=0, channel_multiplier=0, allow_small_or_imprecise_dtypes=True).then_inc(plan_iota, 1)
            g.iota(below.rearrange("p (e f) -> p e f", e=NX), [[1, NX], [-1, NX]], base=0, channel_multiplier=0,
                   allow_small_or_imprecise_dtypes=True).then_inc(plan_iota, 1)
            g.iota(slot_no, [[1, SLOTS]], base=0, channel_multiplier=0, allow_small_or_imprecise_dtypes=True).then_inc(plan_iota, 1)
            pool.wait_ge(pass1_over, 5)

            def body2(J, v):
                s, j, u = tile(J, v, 0, 4, SPAN2)
                if live(s, SLOTS):
                    hold(pool, pool_passed, (gt_done, s - 3), (id_here[u], 16 * (j + 1)))
                    g.indirect_dma_start(xg[u], None, xn_dram, bass.IndirectOffsetOnAxis(ap=id_in[u], axis=0)).then_inc(xg_here[u], 16)

            pipeline(pool, body2, SLOTS, LAG2, SPAN2)
            g.drain().then_inc(pass2_over, 1)
            pool.wait_ge(pass2_over, 5)

            def body3(J, v):
                n, j, u = tile(J, v, 0)
                if live(n, NT):
                    need(pool, f_y_here[u], 16 * TOP * j)
                    for k in range(TOP):
                        g.tensor_copy(f_idx[u][k], row_all[:, bass.ds(n * TOP + k, 1)]).then_inc(f_idx_ready, 1)
                    hold(pool, pool_passed, (f_idx_ready, n * TOP + TOP), (f_c2_done, n - 1))
                    for k in range(TOP):
                        g.indirect_dma_start(f_y[u][k], None, y_dram, bass.IndirectOffsetOnAxis(ap=f_idx[u][k], axis=0)).then_inc(f_y_here[u], 16)

            pipeline(pool, body3, NT, LAG3)

        @block.scalar
        def _(act):
            a = nc.scalar
            act.wait_ge(small_in, 96)
            a.activation(gate[:, :], gate_raw[:, :], ACT.Tanh).then_inc(gate_set, 1)
            act.wait_ge(scale_set, 3)
            a.activation(wq[:, 0, :], wq_raw, ACT.Copy, scale=w_scale[:, 0:1]).then_inc(prep_hi, 1)
            act.wait_ge(wq_in, 16)
            act.dma_start(gu_raw, w_gu_flat).then_inc(raw_in, 16)
            act.dma_start(sgu_raw, s_gu_flat).then_inc(raw_in, 16)
            for i in range(STAGES):
                act.dma_start(stage[i], chunk_src(i)).then_inc(chunk_in[i], 16)

            def body(J, v):
                n, j, u = tile(J, v, 2)
                if live(n, NT):
                    act.wait_ge(xt_done, n + 1)
                    need(act, q_done, n)
                    a.activation(x_hi, bank[0][:, :], ACT.Copy, scale=X_SCALE).then_inc(hi_ready, 1)

                def take_probs(k):
                    n, j, u = tile(J, v, 4)
                    if live(n, NT):
                        act.wait_ge(pt_done, group(n, k))
                        need(act, av_done, group(n, k - 2))
                        a.activation(probs_t[k % 2], bank[4 + k % 2][:, :], ACT.Copy).then_inc(pt_ready, 1)

                def exponent(k):
                    n, j, u = tile(J, v, 3)
                    if live(n, NT):
                        act.wait_ge(shift_done, group(n, k, EC - 1))
                        sc = score[u][:, k * HG * T:(k + 1) * HG * T]
                        a.activation(sc, sc, ACT.Exp).then_inc(exp_done, 1)

                take_probs(0)
                take_probs(1)
                n, j, u = tile(J, v, 7)
                if live(n, NT):
                    act.wait_ge(logit_shift, n + 1)
                    need(act, r_idx_done, n)
                    a.activation(r_exp, bank[1][:, 0:NX], ACT.Exp, bias=logit_neg, accum_out=r_sum).then_inc(r_exp_done, 1)
                exponent(0)
                n, j, u = tile(J, v, 1)
                if live(n, NT):
                    act.wait_ge(ln1_norm, n + 1)
                    need(act, xt_done, n - 1)
                    a.activation(xn[u], x_in[u], ACT.Identity, scale=norm[u][:, 1:2], bias=norm[u][:, 2:3]).then_inc(xn_ready, 1)
                exponent(1)
                take_probs(2)
                take_probs(3)
                n, j, u = tile(J, v, 6)
                if live(n, NT):
                    act.wait_ge(x2t_done, n + 1)
                    need(act, logits_done, n)
                    a.activation(xn2_t, bank[1][:, :], ACT.Copy).then_inc(x2t_ready, 1)
                exponent(2)
                n, j, u = tile(J, v, 3)
                if live(n, NT):
                    act.wait_ge(neg_done, n + 1)
                    for h in range(H - HG, H):
                        sc = score[u][:, h * T:(h + 1) * T]
                        last = a.activation(sc, sc, ACT.Exp, bias=peaks_neg[:, h - H + HG:h - H + HG + 1])
                    last.then_inc(exp_done, 1)
                n, j, u = tile(J, v, 2)
                if live(n, NT):
                    act.wait_ge(q_done, n + 1)
                    need(act, s_done, group(n - 2, EC - 1))
                    for c in range(EC):
                        last = a.activation(q_t[u][:, c * P:(c + 1) * P], bank[0][:, c * P:(c + 1) * P], ACT.Identity,
                                            scale=w_back[:, 0:1], bias=bq_s[:, c:c + 1])
                    last.then_inc(q_ready, 1)

            def beside(it):
                if it < NT:
                    return
                if it == NT:
                    act.wait_ge(scale_set, 6)
                for i in range((it - NT) * per_tail, min((it - NT + 1) * per_tail, len(chunks))):
                    _, dst, at = chunks[i]
                    act.wait_ge(chunk_in[i % STAGES], 16 * (i // STAGES + 1))
                    a.activation(dst[:, 0, at:at + CH], stage[i % STAGES], ACT.Copy, scale=w_scale[:, 1:2]).then_inc(prep_hi, 1)

            pipeline(act, body, NT, LAG1, beside=beside)
            a.drain().then_inc(pass1_over, 1)
            act.wait_ge(pass1_over, 5)

            def body2(J, v):
                s, j, u = tile(J, v, 2, 2, SPAN2)
                if live(s, SLOTS):
                    act.wait_ge(g_ht_done, s + 1)
                    need(act, gd_done, s)
                    a.activation(g_ht, bank[4][:, 0:DX], ACT.Copy).then_inc(g_ht_ready, 1)
                s, j, u = tile(J, v, 3, 2, SPAN2)
                if live(s, SLOTS):
                    act.wait_ge(g_y_ready, s + 1)
                    act.dma_start(y_dram[bass.ds(s * P, P), :], g_y[u]).then_inc(y_out[u], 16)
                s, j, u = tile(J, v, 0, 2, SPAN2)
                if live(s, SLOTS):
                    act.wait_ge(gt_done, s + 1)
                    need(act, gu_done, s - 1)
                    a.activation(g_hi[u], bank[u][:, :], ACT.Copy, scale=X_SCALE).then_inc(g_hi_ready, 1)
                s, j, u = tile(J, v, 1, 2, SPAN2)
                if live(s, SLOTS):
                    act.wait_ge(gu_done, s + 1)
                    need(act, g_h_ready, s - 1)
                    a.activation(g_act[u], bank[2 + u][:, 0:DX], ACT.Silu, scale=w_back[:, 1:2]).then_inc(g_act_ready, 1)

            pipeline(act, body2, SLOTS, LAG2, SPAN2)
            for u in range(2):
                act.wait_ge(y_out[u], 16 * SLOTS // 2)
            a.drain().then_inc(pass2_over, 1)
            act.wait_ge(pass2_over, 5)

            def body3(J, v):
                n, j, u = tile(J, v, 2)
                if live(n, NT):
                    act.wait_ge(f_ht_done, n + 1)
                    need(act, fd_done, n)
                    a.activation(f_ht, bank[6][:, :], ACT.Copy).then_inc(f_ht_ready, 1)
                n, j, u = tile(J, v, 3)
                if live(n, NT):
                    act.wait_ge(f_out_ready, n + 1)
                    act.dma_start(out_tiles[bass.ds(j + u * HALF, 1)].rearrange("a p d -> (a p) d"), f_out[u]).then_inc(f_out_done[u], 16)
                n, j, u = tile(J, v, 0)
                if live(n, NT):
                    act.wait_ge(ft_done, n + 1)
                    need(act, fu_done, n - 1)
                    a.activation(f_hi[u], bank[u][:, :], ACT.Copy, scale=X_SCALE).then_inc(f_hi_ready, 1)
                n, j, u = tile(J, v, 1)
                if live(n, NT):
                    act.wait_ge(fu_done, n + 1)
                    need(act, f_h_ready, n - 1)
                    a.activation(f_act[u], bank[2 + u][:, :], ACT.Silu, scale=w_back[:, 1:2]).then_inc(f_act_ready, 1)

            pipeline(act, body3, NT, LAG3)
            for u in range(2):
                act.wait_ge(f_out_done[u], 16 * HALF)

        @block.vector
        def _(dve):
            d = nc.vector
            d.memset(kbd, 0.0).then_inc(kv_set, 1)
            d.memset(vaug[:, :, :, D:D + 1], 1.0)
            dve.wait_ge(wq_in, 16)
            d.tensor_reduce(peak[:, 0:1], wq_raw, AX.X, ALU.max, apply_absolute_value=True).then_inc(peak_set, 1)

            def scale_of(i, at):
                dve.wait_ge(scale_set, at)
                d.tensor_scalar(w_back[:, i:i + 1], peak_all[:, i:i + 1], TINY, None, ALU.max).then_inc(scale_set, 1)
                dve.wait_ge(scale_set, at + 1)
                bits = w_back[:, i:i + 1].bitcast(I32)
                d.tensor_scalar(bits, bits, EXPONENT, None, ALU.bitwise_and).then_inc(scale_step, 1)
                dve.wait_ge(scale_step, 1 + 2 * i)
                d.reciprocal(w_scale[:, i:i + 1], w_back[:, i:i + 1]).then_inc(scale_step, 1)
                dve.wait_ge(scale_step, 2 + 2 * i)
                d.tensor_scalar(w_back[:, i:i + 1], w_back[:, i:i + 1], 1.0 / (W_TOP * X_SCALE), None, ALU.mult)
                d.tensor_scalar(w_scale[:, i:i + 1], w_scale[:, i:i + 1], W_TOP, None, ALU.mult).then_inc(scale_set, 1)
                dve.wait_ge(scale_set, at + 2)

            scale_of(0, 1)
            dve.wait_ge(prep_hi, 1)
            d.scalar_tensor_tensor(wq[:, 1, :], wq_raw, w_scale[:, 0:1], wq[:, 0, :], ALU.mult, ALU.subtract).then_inc(prep_lo, 1)
            dve.wait_ge(small_in, 96)
            dve.wait_ge(kv_set, 1)
            for c in range(EC):
                dve.wait_ge(kv_mm, 1)
                for b in range(B):
                    for h in range(HG):
                        rows = slice(h * D, (h + 1) * D)
                        d.tensor_scalar(kbd[rows, b, c, h * T:(h + 1) * T], bank[c][rows, b * T:(b + 1) * T],
                                        bk_s[rows, c:c + 1], float(D) ** -0.5, ALU.add, ALU.mult)
            dve.wait_ge(kv_mm, 2)
            for b in range(B):
                last = d.tensor_tensor(vaug[:, b, :, 0:D], bank[4 + b][:, :].rearrange("p (h d) -> p h d", h=H),
                                       bv_s.rearrange("p (h d) -> p h d", h=H), ALU.add)
            last.then_inc(kv_set, 1)
            dve.wait_ge(gate_set, 1)
            dve.wait_ge(const_set, 7)
            dve.wait_ge(seen_zero, 1)

            def body(J, v):
                def maxima(k):
                    n, j, u = tile(J, v, 3)
                    if live(n, NT):
                        hold(dve, dve_passed, (s_done, group(n, k)), (mask_set, n + 1), (pt_done, group(n - 2, k)))
                        for h in range(HG):
                            hh = k * HG + h
                            last = d.tensor_tensor_reduce(score[u][:, hh * T:(hh + 1) * T], bank[2 + k % 2][:, h * T:(h + 1) * T],
                                                          mask_bias[u], 1.0, LOWEST, ALU.add, ALU.max, peaks_of[u][:, hh:hh + 1])
                        last.then_inc(max_done, 1)

                hs = H // 2

                def normalise(half, lag):
                    n, j, u = tile(J, v, lag)
                    if live(n, NT):
                        av = bank[6 + half][:, 0:hs * (D + 1)].rearrange("p (h d) -> p h d", h=hs)
                        inv = inv_sum[:, half * hs:(half + 1) * hs]
                        dve.wait_ge(av_done, group(n, 2 * half + 1))
                        d.reciprocal(inv, av[:, :, D]).then_inc(inv_done[half], 1)
                        dve.wait_ge(inv_done[half], n + 1)
                        d.tensor_tensor(attn[:, half * hs * D:(half + 1) * hs * D].rearrange("p (h d) -> p h d", h=hs), av[:, :, 0:D],
                                        inv.unsqueeze(2).to_broadcast([P, hs, D]), ALU.mult).then_inc(attn_done[half], 1)

                n0, j0, u0 = tile(J, v, 0)
                n5, j5, u5 = tile(J, v, 5)
                n7, j7, u7 = tile(J, v, 7)
                n8, j8, u8 = tile(J, v, 8)
                n, j, u = tile(J, v, 2)
                if live(n, NT):
                    dve.wait_ge(hi_ready, n + 1)
                    d.scalar_tensor_tensor(x_lo, bank[0][:, :], X_SCALE, x_hi, ALU.mult, ALU.subtract).then_inc(lo_ready, 1)
                if live(n8, NT):
                    dve.wait_ge(rank_done, n8 + 1)
                    if live(n7, NT):
                        dve.wait_ge(logits_done, n7 + 1)
                    d.tensor_tensor(at_row, bank[1][:, RANK_AT:RANK_AT + NX], region_at[:, :], ALU.add).then_inc(at_row_done, 1)
                    d.tensor_tensor(seen[:, :], seen[:, :], chosen[u8], ALU.add).then_inc(seen_done, 1)
                if live(n7, NT):
                    dve.wait_ge(logits_done, n7 + 1)
                    d.tensor_reduce(logit_neg, bank[1][:, 0:NX], AX.X, ALU.max, negate=True).then_inc(logit_shift, 1)
                maxima(0)
                maxima(1)
                normalise(1, 5)
                if live(n5, NT):
                    dve.wait_ge(res_here[u5], 16 * (j5 + 1))
                    dve.wait_ge(attn_done[0], n5 + 1)
                    dve.wait_ge(attn_done[1], n5 + 1)
                    need(dve, x1_out[u5], 16 * j5)
                    d.scalar_tensor_tensor(x1[u5], attn, gate[:, 0:1], x_res[u5], ALU.mult, ALU.add).then_inc(x1_ready, 1)
                n, j, u = tile(J, v, 6)
                if live(n, NT):
                    dve.wait_ge(ln2_std, n + 1)
                    need(dve, x2t_done, n - 1)
                    need(dve, xn2_out[u], 16 * j)
                    d.tensor_scalar(xn2[u], x1[u], mv2[u][:, 0:1], norm2[u][:, 1:2], ALU.subtract, ALU.mult).then_inc(xn2_ready, 1)
                maxima(2)
                if live(n5, NT):
                    dve.wait_ge(x1_ready, n5 + 1)
                    d.bn_stats(stats2[u5], x1[u5]).then_inc(ln2_stats, 1)
                maxima(EC - 1)
                if live(n7, NT):
                    hold(dve, dve_passed, (r_exp_done, n7 + 1))
                    d.max(r_top, r_exp).then_inc(r_top_done, 1)
                    d.reciprocal(r_inv, r_sum).then_inc(r_inv_done, 1)
                n, j, u = tile(J, v, 3)
                if live(n, NT):
                    dve.wait_ge(max_done, group(n, EC - 1))
                    need(dve, exp_done, group(n - 1, EC - 1))
                    d.tensor_scalar(peaks_neg, peaks_of[u][:, H - HG:H], -1.0, None, ALU.mult).then_inc(neg_done, 1)
                if live(n5, NT):
                    hold(dve, dve_passed, (ln2_stats, n5 + 1))
                    d.bn_aggr(mv2[u5], stats2[u5]).then_inc(ln2_mv, 1)
                if live(n7, NT):
                    hold(dve, dve_passed, (r_top_done, n7 + 1))
                    d.max_index(r_idx, r_top, r_exp).then_inc(r_idx_done, 1)
                if live(n8, NT):
                    dve.wait_ge(at_row_done, n8 + 1)
                    d.tensor_tensor_reduce(junk[0], at_row, first[u8], 1.0, 0.0, ALU.mult, ALU.add, row_f[:, 0:1])
                    d.tensor_tensor_reduce(junk[1], at_row, second[u8], 1.0, 0.0, ALU.mult, ALU.add, row_f[:, 1:2]).then_inc(row_f_done, 1)
                if live(n7, NT):
                    dve.wait_ge(r_idx_done, n7 + 1)
                    d.tensor_scalar(first[u7], expert_no[:, :], r_idx[:, 0:1], None, ALU.is_equal)
                    d.tensor_scalar(second[u7], expert_no[:, :], r_idx[:, 1:2], None, ALU.is_equal).then_inc(first_done, 1)
                    dve.wait_ge(r_inv_done, n7 + 1)
                    d.tensor_scalar(prob_all[:, bass.ds(n7 * TOP, TOP)], r_top[:, 0:TOP], r_inv, None, ALU.mult)
                    dve.wait_ge(first_done, n7 + 1)
                    d.tensor_tensor(chosen[u7], first[u7], second[u7], ALU.add).then_inc(chosen_done, 1)
                if live(n0, NT):
                    dve.wait_ge(x_here[u0], 16 * (j0 + 1))
                    d.bn_stats(stats[u0], x_in[u0]).then_inc(ln1_stats, 1)
                if live(n8, NT):
                    dve.wait_ge(row_f_done, n8 + 1)
                    need(dve, rows_out[u8], 16 * TOP * j8)
                    d.tensor_copy(row_i[u8], row_f).then_inc(row_ready, 1)
                    d.tensor_copy(row_list[:, bass.ds(n8 * TOP, TOP)], row_f)
                if live(n0, NT):
                    hold(dve, dve_passed, (ln1_stats, n0 + 1))
                    d.bn_aggr(mv[u0], stats[u0]).then_inc(ln1_mv, 1)
                normalise(0, 4)

            def beside(it):
                if it < HEAD1:
                    if it == 0:
                        dve.wait_ge(raw_in, 32)
                    for i in range(it * len(chunks) // HEAD1, (it + 1) * len(chunks) // HEAD1):
                        raw, _, at = chunks[i]
                        last = d.tensor_reduce(peak[:, 1 + i:2 + i], raw[:, at:at + CH], AX.X, ALU.max, apply_absolute_value=True)
                        last.then_inc(peak_step, 1)
                    if it == HEAD1 - 1:
                        dve.wait_ge(peak_step, len(chunks))
                        d.tensor_reduce(peak[:, 15:16], peak[:, 1:1 + len(chunks)], AX.X, ALU.max).then_inc(peak_set, 1)
                    return
                if it == NT:
                    scale_of(1, 4)
                for i in range((it - NT) * per_tail, min((it - NT + 1) * per_tail, len(chunks))):
                    _, dst, at = chunks[i]
                    dve.wait_ge(prep_hi, 2 + i)
                    d.scalar_tensor_tensor(dst[:, 1, at:at + CH], stage[i % STAGES], w_scale[:, 1:2], dst[:, 0, at:at + CH],
                                           ALU.mult, ALU.subtract).then_inc(prep_lo, 1)

            pipeline(dve, body, NT, LAG1, beside=beside)
            d.drain().then_inc(pass1_over, 1)

            steps = [0]

            def link(ins):
                steps[0] += 1
                ins.then_inc(plan_step, 1)
                dve.wait_ge(plan_step, steps[0])

            dve.wait_ge(plan_iota, 3)
            dve.wait_ge(counts_done, 1)
            le = below.rearrange("p (e f) -> p e f", e=NX)
            r3 = reached.rearrange("p (e t) -> p e t", e=NX)
            link(d.tensor_tensor(r3, bank[0][:, 0:NX].unsqueeze(2).to_broadcast([P, NX, NT]),
                                 step_at.unsqueeze(1).to_broadcast([P, NX, NT]), ALU.is_gt))
            link(d.tensor_reduce(n_tiles, r3, AX.X, ALU.add))
            link(d.tensor_scalar(below, below, 0.0, None, ALU.is_ge))
            link(d.tensor_tensor(le, le, n_tiles.unsqueeze(1).to_broadcast([P, NX, NX]), ALU.mult))
            link(d.tensor_reduce(upto, le, AX.X, ALU.add))
            p3 = passed.rearrange("p (s e) -> p s e", s=SLOTS)
            pn = passed_n.rearrange("p (s e) -> p s e", s=SLOTS)
            link(d.tensor_tensor(p3, slot_no.unsqueeze(2).to_broadcast([P, SLOTS, NX]),
                                 upto.unsqueeze(1).to_broadcast([P, SLOTS, NX]), ALU.is_ge))
            link(d.tensor_reduce(expert_f, p3, AX.X, ALU.add))
            link(d.tensor_tensor(pn, p3, n_tiles.unsqueeze(1).to_broadcast([P, SLOTS, NX]), ALU.mult))
            link(d.tensor_reduce(base_f, pn, AX.X, ALU.add))
            link(d.tensor_tensor(row_sf, slot_no, base_f, ALU.subtract))
            link(d.tensor_scalar(row_sf, row_sf, float(P), None, ALU.mult))
            link(d.scalar_tensor_tensor(row_sf, expert_f, float(REGION), row_sf, ALU.mult, ALU.add))
            d.tensor_copy(slot_row[:, :], row_sf).then_inc(plan_ready, 1)
            link(d.tensor_scalar(expert_f, expert_f, float(NX - 1), None, ALU.min))
            d.tensor_copy(slot_expert[:, :], expert_f).then_inc(plan_ready, 1)
            l3 = later.rearrange("p (r e) -> p r e", e=NX - 1)
            link(d.tensor_scalar(moved, n_tiles[:, 0:NX - 1], float(P), -float(REGION), ALU.mult, ALU.add))
            link(d.tensor_tensor(l3, row_list[:, :].unsqueeze(2).to_broadcast([P, NT * TOP, NX - 1]),
                                 region_at[:, 1:NX].unsqueeze(1).to_broadcast([P, NT * TOP, NX - 1]), ALU.is_ge))
            link(d.tensor_tensor(l3, l3, moved.unsqueeze(1).to_broadcast([P, NT * TOP, NX - 1]), ALU.mult))
            link(d.tensor_reduce(row_slots, l3, AX.X, ALU.add))
            link(d.tensor_tensor(row_slots, row_slots, row_list[:, :], ALU.add))
            link(d.tensor_copy(row_all[:, :], row_slots))
            dve.wait_ge(pass1_over, 5)

            def body2(J, v):
                s, j, u = tile(J, v, 0, 2, SPAN2)
                if live(s, SLOTS):
                    dve.wait_ge(g_hi_ready, s + 1)
                    need(dve, gu_done, s - 1)
                    d.scalar_tensor_tensor(g_lo[u], bank[u][:, :], X_SCALE, g_hi[u], ALU.mult, ALU.subtract).then_inc(g_lo_ready, 1)
                s, j, u = tile(J, v, 1, 2, SPAN2)
                if live(s, SLOTS):
                    dve.wait_ge(g_act_ready, s + 1)
                    need(dve, g_ht_done, s - 1)
                    d.scalar_tensor_tensor(g_h[u], bank[2 + u][:, DX:2 * DX], w_back[:, 1:2], g_act[u], ALU.mult, ALU.mult).then_inc(g_h_ready, 1)
                s, j, u = tile(J, v, 2, 2, SPAN2)
                if live(s, SLOTS):
                    dve.wait_ge(gd_done, s + 1)
                    need(dve, y_out[u], 16 * j)
                    d.tensor_copy(g_y[u], bank[6 + u][:, :]).then_inc(g_y_ready, 1)

            pipeline(dve, body2, SLOTS, LAG2, SPAN2)
            d.drain().then_inc(pass2_over, 1)
            dve.wait_ge(pass2_over, 5)

            def body3(J, v):
                n, j, u = tile(J, v, 0)
                if live(n, NT):
                    dve.wait_ge(f_hi_ready, n + 1)
                    need(dve, fu_done, n - 1)
                    d.scalar_tensor_tensor(f_lo[u], bank[u][:, :], X_SCALE, f_hi[u], ALU.mult, ALU.subtract).then_inc(f_lo_ready, 1)
                n, j, u = tile(J, v, 1)
                if live(n, NT):
                    dve.wait_ge(f_act_ready, n + 1)
                    need(dve, f_ht_done, n - 1)
                    d.scalar_tensor_tensor(f_h[u], bank[4 + u][:, :], w_back[:, 1:2], f_act[u], ALU.mult, ALU.mult).then_inc(f_h_ready, 1)
                n, j, u = tile(J, v, 2)
                if live(n, NT):
                    dve.wait_ge(fd_done, n + 1)
                    dve.wait_ge(f_y_here[u], 16 * TOP * (j + 1))
                    d.scalar_tensor_tensor(f_c1, f_y[u][0], prob_all[:, bass.ds(n * TOP, 1)], bank[7][:, :], ALU.mult, ALU.add).then_inc(f_c1_done, 1)
                    dve.wait_ge(f_c1_done, n + 1)
                    d.scalar_tensor_tensor(f_c2, f_y[u][1], prob_all[:, bass.ds(n * TOP + 1, 1)], f_c1, ALU.mult, ALU.add).then_inc(f_c2_done, 1)
                    dve.wait_ge(f_c2_done, n + 1)
                    dve.wait_ge(f_x1_here[u], 16 * (j + 1))
                    need(dve, f_out_done[u], 16 * j)
                    d.scalar_tensor_tensor(f_out[u], f_c2, gate[:, 1:2], f_x1[u], ALU.mult, ALU.add).then_inc(f_out_ready, 1)

            pipeline(dve, body3, NT, LAG3)

        @block.tensor
        def _(pe):
            t = nc.tensor

            def transposes(dst, src, count):
                for c in range(count):
                    last = t.transpose(dst[:, c * P:(c + 1) * P], src[:, c * P:(c + 1) * P], ident[:, :])
                return last

            def split_product(dst, hi, lo, w_hi, w_lo):
                for c in range(EC):
                    rows = slice(c * P, (c + 1) * P)
                    t.matmul(dst, hi[:, rows], w_hi(c), start=(c == 0), stop=False)
                    t.matmul(dst, hi[:, rows], w_lo(c), start=False, stop=False)
                    last = t.matmul(dst, lo[:, rows], w_hi(c), start=False, stop=(c == EC - 1))
                return last

            pe.wait_ge(kv_in, 48)
            for co in range(EC):
                for ci in range(EC):
                    last = t.matmul(bank[co][:, 0:B * T], wk_s[:, ci, co * P:(co + 1) * P], ctx_s[:, ci, :],
                                    start=(ci == 0), stop=(ci == EC - 1))
            last.then_inc(kv_mm, 1)
            for b in range(B):
                for ci in range(EC):
                    last = t.matmul(bank[4 + b][:, :], ctx_s[:, ci, b * T:(b + 1) * T], wv_s[:, ci, :],
                                    start=(ci == 0), stop=(ci == EC - 1))
            last.then_inc(kv_mm, 1)
            pe.wait_ge(const_set, 7)
            pe.wait_ge(kv_set, 2)
            pe.wait_ge(prep_lo, 1)

            def body(J, v):
                n, j, u = tile(J, v, 2)
                if live(n, NT):
                    pe.wait_ge(xn_ready, n + 1)
                    need(pe, q_ready, n)
                    transposes(bank[0], xn[u], EC).then_inc(xt_done, 1)

                def scores(k):
                    n, j, u = tile(J, v, 3)
                    if live(n, NT):
                        pe.wait_ge(q_ready, n + 1)
                        need(pe, max_done, group(n, k - 2))
                        t.matmul(bank[2 + k % 2][:, :], q_t[u][:, k * P:(k + 1) * P], kbd[:, u, k, :],
                                 start=True, stop=True).then_inc(s_done, 1)

                def turn_probs(k):
                    n, j, u = tile(J, v, 4)
                    if live(n, NT):
                        pe.wait_ge(exp_done, group(n, k))
                        need(pe, pt_ready, group(n, k - 2))
                        transposes(bank[4 + k % 2], score[u][:, k * HG * T:(k + 1) * HG * T], HG).then_inc(pt_done, 1)

                def mix_values(k):
                    n, j, u = tile(J, v, 4)
                    if live(n, NT):
                        pe.wait_ge(pt_ready, group(n, k))
                        half = k // 2
                        need(pe, attn_done[half], n)
                        for h in range(HG):
                            at = (k % 2 * HG + h) * (D + 1)
                            last = t.matmul(bank[6 + half][:, at:at + D + 1], probs_t[k % 2][:, h * P:(h + 1) * P],
                                            vaug[:, u, k * HG + h, :], start=True, stop=True)
                        last.then_inc(av_done, 1)

                def queries(chunks):
                    n, j, u = tile(J, v, 2)
                    if live(n, NT):
                        pe.wait_ge(lo_ready, n + 1)
                        for co in chunks:
                            dst = bank[0][:, co * P:(co + 1) * P]
                            for ci in range(EC):
                                at = ci * E + co * P
                                xs = slice(ci * P, (ci + 1) * P)
                                t.matmul(dst, wq[:, 0, at:at + P], x_hi[:, xs], start=(ci == 0), stop=False)
                                t.matmul(dst, wq[:, 0, at:at + P], x_lo[:, xs], start=False, stop=False)
                                last = t.matmul(dst, wq[:, 1, at:at + P], x_hi[:, xs], start=False, stop=(ci == EC - 1))
                        if chunks[-1] == EC - 1:
                            last.then_inc(q_done, 1)

                turn_probs(0)
                turn_probs(1)
                scores(0)
                scores(1)
                mix_values(0)
                scores(2)
                mix_values(1)
                scores(3)
                turn_probs(2)
                turn_probs(3)
                n, j, u = tile(J, v, 6)
                if live(n, NT):
                    pe.wait_ge(xn2_ready, n + 1)
                    need(pe, r_exp_done, n)
                    need(pe, at_row_done, n - 1)
                    transposes(bank[1], xn2[u], EC).then_inc(x2t_done, 1)
                queries((0, 1))
                mix_values(2)
                queries((2, 3))
                mix_values(3)
                n6, j6, u6 = tile(J, v, 6)
                if live(n6, NT):
                    pe.wait_ge(x2t_ready, n6 + 1)
                n, j, u = tile(J, v, 7)
                if live(n, NT):
                    pe.wait_ge(chosen_done, n + 1)
                    need(pe, seen_done, n)
                    ranks = bank[1][:, RANK_AT:RANK_AT + NX]
                    t.matmul(ranks, before[:, :], chosen[u], start=True, stop=False)
                    t.matmul(ranks, ones[:, :], seen[:, :], start=False, stop=True).then_inc(rank_done, 1)
                if live(n6, NT):
                    for c in range(EC):
                        last = t.matmul(bank[1][:, 0:NX], xn2_t[:, c * P:(c + 1) * P], router_s[:, c, :],
                                        start=(c == 0), stop=(c == EC - 1))
                    last.then_inc(logits_done, 1)

            pipeline(pe, body, NT, LAG1)
            pe.wait_ge(seen_done, NT)
            pe.wait_ge(q_ready, NT)
            t.matmul(bank[0][:, 0:NX], ones[:, :], seen[:, :], start=True, stop=True).then_inc(counts_done, 1)
            t.drain().then_inc(pass1_over, 1)
            pe.wait_ge(pass1_over, 5)
            pe.wait_ge(down_in, 16)

            def body2(J, v):
                s, j, u = tile(J, v, 2, 2, SPAN2)
                if live(s, SLOTS):
                    pe.wait_ge(g_h_ready, s + 1)
                    need(pe, g_ht_ready, s)
                    transposes(bank[4], g_h[u], DX // P).then_inc(g_ht_done, 1)
                s, j, u = tile(J, v, 0, 4, SPAN2)
                if live(s, SLOTS):
                    pe.wait_ge(xg_here[u], 16 * (j + 1))
                    need(pe, g_lo_ready, s - 1)
                    transposes(bank[u % 2], xg[u], EC).then_inc(gt_done, 1)
                s, j, u = tile(J, v, 1, 2, SPAN2)
                if live(s, SLOTS):
                    e = pe.value_load(slot_expert[0:1, bass.ds(s, 1)], min_val=0, max_val=NX - 1)
                    pe.wait_ge(g_lo_ready, s + 1)
                    need(pe, g_h_ready, s - 1)
                    w = 2 * DX
                    split_product(bank[2 + u][:, :], g_hi[u], g_lo[u],
                                  lambda c: gu_flat[:, bass.ds(e * (EC * w) + c * w, w)],
                                  lambda c: gu_flat[:, bass.ds(e * (EC * w) + (GU + c * w), w)]).then_inc(gu_done, 1)
                s, j, u = tile(J, v, 2, 2, SPAN2)
                if live(s, SLOTS):
                    e = pe.value_load(slot_expert[0:1, bass.ds(s, 1)], min_val=0, max_val=NX - 1)
                    pe.wait_ge(g_ht_ready, s + 1)
                    need(pe, g_y_ready, s - 1)
                    nd = DX // P
                    for c in range(nd):
                        last = t.matmul(bank[6 + u][:, :], g_ht[:, c * P:(c + 1) * P], wd[:, bass.ds(e * (nd * E) + c * E, E)],
                                        start=(c == 0), stop=(c == nd - 1))
                    last.then_inc(gd_done, 1)

            pipeline(pe, body2, SLOTS, LAG2, SPAN2)
            t.drain().then_inc(pass2_over, 1)
            pe.wait_ge(pass2_over, 5)
            pe.wait_ge(swd_in, 16)

            def body3(J, v):
                n, j, u = tile(J, v, 2)
                if live(n, NT):
                    pe.wait_ge(f_h_ready, n + 1)
                    need(pe, f_ht_ready, n)
                    transposes(bank[6], f_h[u], DS // P).then_inc(f_ht_done, 1)
                n, j, u = tile(J, v, 0)
                if live(n, NT):
                    pe.wait_ge(f_x_here[u], 16 * (j + 1))
                    need(pe, f_lo_ready, n - 1)
                    transposes(bank[u], f_x[u], EC).then_inc(ft_done, 1)
                n, j, u = tile(J, v, 1)
                if live(n, NT):
                    pe.wait_ge(f_lo_ready, n + 1)
                    need(pe, f_h_ready, n - 1)
                    for part in range(2):
                        last = split_product(bank[2 + 2 * part + u][:, :], f_hi[u], f_lo[u],
                                             lambda c: sgu[:, 0, (2 * c + part) * DS:(2 * c + part + 1) * DS],
                                             lambda c: sgu[:, 1, (2 * c + part) * DS:(2 * c + part + 1) * DS])
                    last.then_inc(fu_done, 1)
                n, j, u = tile(J, v, 2)
                if live(n, NT):
                    pe.wait_ge(f_ht_ready, n + 1)
                    need(pe, f_c1_done, n)
                    for c in range(DS // P):
                        last = t.matmul(bank[7][:, :], f_ht[:, c * P:(c + 1) * P], swd[:, c, :],
                                        start=(c == 0), stop=(c == DS // P - 1))
                    last.then_inc(fd_done, 1)

            pipeline(pe, body3, NT, LAG3)


def kernel(**inputs):
    import concourse.bacc as bacc
    from concourse.bass_utils import run_bass_kernel_spmd

    got = {k: np.asarray(v) for k, v in inputs.items()}

    def rows(w, *lead):
        w = w.reshape(*w.shape[:-2], w.shape[-2] // P, P, w.shape[-1])
        return np.ascontiguousarray(np.moveaxis(w, -2, 0))

    def cols(b):
        return np.ascontiguousarray(b.reshape(EC, P).T)

    gate_up = np.concatenate([got["L0_ffn_experts_gate"], got["L0_ffn_experts_up"]], axis=-1)
    shared_gate_up = np.concatenate([got["L0_ffn_shared_gate"], got["L0_ffn_shared_up"]], axis=-1)
    arrays = {
        "x": got["x"],
        "ctx_t": rows(got["ctx_1024"].reshape(B * T, E).T),
        "pad": np.broadcast_to(got["mask_Bx1x1xS2_ik0"].reshape(1, B, T), (P, B, T)),
        "sub": got["mask_1x1xSxS2_ik0"],
        "gates": np.broadcast_to(np.concatenate([got["g_xattn"], got["g_ffn"]]).reshape(1, 2), (P, 2)),
        "wq_t": rows(got["L0_xattn_Wq"].T),
        "wk_t": rows(got["L0_xattn_Wk"].T),
        "wv_t": rows(got["L0_xattn_Wv"].T),
        "bq": cols(got["L0_xattn_bq"]),
        "bk": cols(got["L0_xattn_bk"]),
        "bv": np.broadcast_to(got["L0_xattn_bv"].reshape(1, E), (P, E)),
        "router": rows(got["L0_ffn_router"]),
        "w_gu": rows(gate_up),
        "w_down": rows(got["L0_ffn_experts_down"]),
        "s_gu": rows(shared_gate_up),
        "s_down": rows(got["L0_ffn_shared_down"]),
    }
    arrays = {f"in_{k}": np.ascontiguousarray(v) for k, v in arrays.items()}
    nc = bacc.Bacc("TRN2", target_bir_lowering=False, num_devices=1)
    args = [nc.dram_tensor(k, v.shape, mybir.dt.from_np(v.dtype), kind="ExternalInput").ap() for k, v in arrays.items()]
    out = nc.dram_tensor("out", (B, S, E), F32, kind="ExternalOutput").ap()
    build(nc, *args, out)
    r = run_bass_kernel_spmd(nc, [arrays], core_ids=[0])
    return r.results[0]["out"]
```

```python
from contextlib import ExitStack

import concourse.bass as bass
import numpy as np
from concourse import mybir

F32, F16 = mybir.dt.float32, mybir.dt.float16
I32, U32 = mybir.dt.int32, mybir.dt.uint32
ALU = mybir.AluOpType
ACT = mybir.ActivationFunctionType
AX = mybir.AxisListType
RMAX = bass.bass_isa.ReduceOp.max

P = 128
B, S, E = 2, 2048, 512
T = 128
H, D = 16, 32
NX, DX, DS, TOP = 8, 256, 512, 2
TOK = B * S
NT = TOK // P
EC = E // P
HG = H // EC
REGION = TOK
SLOTS = TOK * TOP // P + NX
LISTS = (NX + 1) * REGION
EPS = 1e-5
MASKED = -1e30
LOWEST = -3e38
X_SCALE = 1024.0
W_TOP = 16384.0
H_TOP = 16384.0
TINY = 2.0 ** -100
EXPONENT = 0x7F800000


def build(nc, x, ctx_t, pad, sub, gates, wq_t, wk_t, wv_t, bq, bk, bv, router, w_gu, w_down, s_gu, s_down, out):
    x_tiles = x.rearrange("b (j p) d -> (b j) p d", p=P)
    out_tiles = out.rearrange("b (j p) d -> (b j) p d", p=P)
    sub_tiles = sub.rearrange("a b (j p) t -> (a b j) p t", p=P)
    HALF = NT // B

    x1_dram = nc.dram_tensor("x1_rows", [TOK, E], F32).ap()
    xn_dram = nc.dram_tensor("normed_rows", [TOK, E], F32).ap()
    list_dram = nc.dram_tensor("token_of_row", [LISTS, 1], I32).ap()
    y_dram = nc.dram_tensor("expert_rows", [SLOTS * P, E], F32).ap()

    with ExitStack() as ctx:
        def sb(name, shape, dt=F32):
            return ctx.enter_context(nc.sbuf_tensor(name, shape, dt))

        def sems(names):
            return [ctx.enter_context(nc.semaphore(n)) for n in names.split()]

        bank = [ctx.enter_context(nc.psum_tensor(f"bank{i}", [P, 512], F32)) for i in range(8)]

        CH = 2048
        EXPERT_CHUNKS, SHARED_CHUNKS = NX * EC * 2 * DX // CH, EC * 2 * DS // CH
        CHUNKS = EXPERT_CHUNKS + SHARED_CHUNKS
        XD = DX // P * E
        DOWN_CHUNKS = NX * XD // CH
        ALL_CHUNKS = CHUNKS + DOWN_CHUNKS
        weights = sb("weights", [P, ALL_CHUNKS * CH])
        gu = weights[:, :].bitcast(F16)
        DOWN_AT = CHUNKS * 2 * CH

        def raw(i):
            return weights[:, bass.ds((i + 1) * CH, CH)]

        def halves(i):
            return [gu[:, bass.ds((2 * i + k) * CH, CH)] for k in range(2)]

        def by_expert(w):
            return w.rearrange("p (x n) -> p x n", n=XD)

        def down_halves(i):
            by_half = gu[:, 2 * i * CH:2 * (i + 1) * CH].rearrange("p (x a n) -> p x a n", a=2, n=XD)
            return by_half[:, :, 0], by_half[:, :, 1]

        wq_raw = weights[:, 0:CH]

        ident = sb("ident", [P, P])
        ident16 = sb("ident16", [P, P], F16)
        before = sb("before", [P, P], F16)
        ones = sb("ones", [P, P], F16)
        pad_raw = sb("pad_raw", [P, B, T], I32)
        pad_bias = sb("pad_bias", [P, B, T])
        pad_keep = sb("pad_keep", [P, B, T])
        gate_raw = sb("gate_raw", [P, 2])
        gate = sb("gate", [P, 2])
        bq_s = sb("bq_s", [P, EC])
        bk_s = sb("bk_s", [P, EC])
        router_s = sb("router_s", [P, EC, NX])
        half_power = sb("half_power", [P, 1])
        peak = sb("peak", [P, 20])
        peak_all = sb("peak_all", [P, 4])
        w_scale = sb("w_scale", [P, 4])
        w_back = sb("w_back", [P, 4])
        expert_no = sb("expert_no", [P, NX])
        region_at = sb("region_at", [P, NX])
        token_no = sb("token_no", [P, HALF, B], I32)
        step_at = sb("step_at", [P, NT])
        upto_e = sb("upto_e", [P, NX, NX])
        slot_no = sb("slot_no", [P, SLOTS])
        zeros_i = sb("zeros_i", [P, LISTS // P], I32)
        seen = sb("seen", [P, NX], F16)
        prob_all = sb("prob_all", [P, NT * TOP])
        row_list = sb("row_list", [P, NT * TOP])
        row_all = sb("row_all", [P, NT * TOP], U32)
        slot_row = sb("slot_row", [P, SLOTS], I32)
        slot_expert = sb("slot_expert", [P, SLOTS], I32)

        ARENA = 21 * 1024
        arena = sb("arena", [P, ARENA])
        top = [0]

        def carve(cols):
            top[0] += cols
            assert top[0] <= ARENA, top[0]
            return arena[:, top[0] - cols:top[0]]

        wq = carve(EC * E).bitcast(F16).rearrange("p (a n) -> p a n", a=2)
        kbd = carve(B * EC * HG * T).rearrange("p (b c n) -> p b c n", b=B, c=EC)
        vaug = carve(B * H * (D + 1)).rearrange("p (b h d) -> p b h d", b=B, h=H)
        score = [carve(H * T) for _ in range(2)]
        wk_s = score[0].rearrange("p (c n) -> p c n", c=EC)
        wv_s = score[1].rearrange("p (c n) -> p c n", c=EC)
        probs_t = [carve(HG * T) for _ in range(2)]
        x_in = [carve(E) for _ in range(2)]
        xn = [carve(E) for _ in range(2)]
        last_raw = arena[:, top[0] - 4 * E:top[0]]
        x_res = [carve(E) for _ in range(2)]
        x_hi, x_lo = carve(E // 2).bitcast(F16), carve(E // 2).bitcast(F16)
        q_t = [carve(E) for _ in range(2)]
        attn = carve(E)
        x1 = [carve(E) for _ in range(2)]
        xn2 = [carve(E) for _ in range(2)]
        xn2_t = carve(E)
        bv_s = attn
        ctx_s = arena[:, top[0] - 3 * E:top[0] - E].rearrange("p (c n) -> p c n", c=EC)
        sub_raw = carve(T).bitcast(I32)
        sub_bias = carve(T)
        mask_bias = [carve(T) for _ in range(2)]
        peaks_of = [carve(H) for _ in range(2)]
        peaks_neg = carve(HG)
        stats = [carve(6) for _ in range(2)]
        stats2 = [carve(6) for _ in range(2)]
        mv, mv2 = [carve(2) for _ in range(2)], [carve(2) for _ in range(2)]
        norm, norm2 = [carve(3) for _ in range(2)], [carve(3) for _ in range(2)]
        inv_sum = carve(H)
        logit_top, logit_neg = carve(NX), carve(1)
        r_exp, r_sum, r_inv, r_prob, r_top = carve(NX), carve(1), carve(1), carve(NX), carve(NX)
        r_idx = carve(NX).bitcast(U32)
        r_idxf = carve(TOP)
        first = [carve(NX) for _ in range(2)]
        second = [carve(NX) for _ in range(2)]
        chosen = [carve(NX // 2).bitcast(F16) for _ in range(2)]
        at_row = carve(NX)
        junk = [carve(NX) for _ in range(2)]
        row_f = carve(TOP)
        row_i = [carve(TOP).bitcast(U32) for _ in range(2)]
        tok_i = [carve(1).bitcast(I32) for _ in range(2)]

        top[0] = 0
        SD = DS // P * E
        swd = carve(SD).bitcast(F16).rearrange("p (a n) -> p a n", a=2)
        id_in = [carve(1).bitcast(I32) for _ in range(4)]
        xg = [carve(E) for _ in range(4)]
        g_hi = [carve(E // 2).bitcast(F16) for _ in range(2)]
        g_lo = [carve(E // 2).bitcast(F16) for _ in range(2)]
        g_act = [carve(DX) for _ in range(2)]
        g_h = [carve(DX) for _ in range(2)]
        g_h_hi = [carve(DX // 2).bitcast(F16) for _ in range(2)]
        g_h_lo = [carve(DX // 2).bitcast(F16) for _ in range(2)]
        g_top = carve(1)
        g_size = [carve(1) for _ in range(4)]
        g_scale = [carve(1) for _ in range(2)]
        g_ht = carve(DX).bitcast(F16)
        g_y = [carve(E) for _ in range(2)]
        PASS2_END = top[0]

        SCORES_END = EC * E + B * EC * HG * T + B * H * (D + 1) + 2 * H * T
        PLAN = NX * NT + 3 * NX + NX * NX + 2 * SLOTS * NX + 2 * SLOTS + NT * TOP * NX
        top[0] = SCORES_END - PLAN
        assert top[0] >= PASS2_END
        reached = carve(NX * NT)
        n_tiles, upto, ahead = carve(NX), carve(NX), carve(NX)
        below = carve(NX * NX)
        passed = carve(SLOTS * NX)
        passed_n = carve(SLOTS * NX)
        expert_f, row_sf = carve(SLOTS), carve(SLOTS)
        later = carve(NT * TOP * (NX - 1))
        row_slots = carve(NT * TOP)
        swd_raw = carve(SD)

        top[0] = PASS2_END
        f_x = [carve(E) for _ in range(2)]
        f_x1 = [carve(E) for _ in range(2)]
        f_idx = [[carve(1).bitcast(U32) for _ in range(TOP)] for _ in range(2)]
        f_y = [[carve(E) for _ in range(TOP)] for _ in range(2)]
        f_hi = [carve(E // 2).bitcast(F16) for _ in range(2)]
        f_lo = [carve(E // 2).bitcast(F16) for _ in range(2)]
        f_act = [carve(DS) for _ in range(2)]
        f_h = [carve(DS) for _ in range(2)]
        f_h_hi = [carve(DS // 2).bitcast(F16) for _ in range(2)]
        f_h_lo = [carve(DS // 2).bitcast(F16) for _ in range(2)]
        f_top = carve(1)
        f_size = [carve(1) for _ in range(4)]
        f_scale = [carve(1) for _ in range(2)]
        f_back = [carve(1) for _ in range(4)]
        f_ht = carve(DS).bitcast(F16)
        f_c0, f_c1, f_c2 = carve(E), carve(E), carve(E)
        f_out = [carve(E) for _ in range(2)]

        small_in, kv_in, wq_in, swd_in = sems("small_in kv_in wq_in swd_in")
        chunk_in = sems(" ".join(f"chunk_in{i}" for i in range(ALL_CHUNKS)))
        again_in = sems(" ".join(f"again_in{i}" for i in range(DOWN_CHUNKS)))
        x_here, res_here, xn2_out, x1_out, rows_out = (sems(f"{n}0 {n}1") for n in ("x_here", "res_here", "xn2_out", "x1_out", "rows_out"))
        sub_here, list_zero = sems("sub_here list_zero")
        id_here, xg_here = (sems(f"{n}0 {n}1 {n}2 {n}3") for n in ("id_here", "xg_here"))
        y_out = sems("y_out0 y_out1")
        f_x_here, f_x1_here, f_y_here, f_out_done = (sems(f"{n}0 {n}1") for n in ("f_x_here", "f_x1_here", "f_y_here", "f_out_done"))
        dve_passed, pool_passed, peak_step = sems("dve_passed pool_passed peak_step")
        const_set, pool_set, peak_set, scale_set, prep_hi, prep_lo, kv_mm, kv_set, gate_set = sems(
            "const_set pool_set peak_set scale_set prep_hi prep_lo kv_mm kv_set gate_set")
        ln1_stats, ln1_mv, ln1_eps, ln1_std, ln1_norm, xn_ready = sems("ln1_stats ln1_mv ln1_eps ln1_std ln1_norm xn_ready")
        xt_done, hi_ready, lo_ready, q_done, q_ready = sems("xt_done hi_ready lo_ready q_done q_ready")
        sub_set, mask_half, mask_set = sems("sub_set mask_half mask_set")
        s_done, max_done, shift_done, exp_done, pt_done, pt_ready, av_done, neg_done = sems(
            "s_done max_done shift_done exp_done pt_done pt_ready av_done neg_done")
        inv_done, attn_done = sems("inv_done0 inv_done1"), sems("attn_done0 attn_done1")
        x1_ready, ln2_stats, ln2_mv, ln2_eps, ln2_std, xn2_ready = sems(
            "x1_ready ln2_stats ln2_mv ln2_eps ln2_std xn2_ready")
        x2t_done, x2t_ready, logits_done, logit_shift, r_exp_done, r_inv_done, r_top_done = sems(
            "x2t_done x2t_ready logits_done logit_shift r_exp_done r_inv_done r_top_done")
        r_idx_done, first_done, chosen_done, rank_done, at_row_done, row_f_done, row_ready, tok_ready, seen_done, seen_zero = sems(
            "r_idx_done first_done chosen_done rank_done at_row_done row_f_done row_ready tok_ready seen_done seen_zero")
        pass1_over, counts_done, scale_step, plan_step, plan_ready = sems(
            "pass1_over counts_done scale_step plan_step plan_ready")
        gt_done, g_hi_ready, g_lo_ready, gu_done, g_act_ready, g_h_ready, g_top_done, g_size_done, g_scale_done, g_h_hi_done, g_h_lo_done, g_ht_done, g_ht_ready, gd_done, g_y_ready = sems(
            "gt_done g_hi_ready g_lo_ready gu_done g_act_ready g_h_ready g_top_done g_size_done g_scale_done g_h_hi_done g_h_lo_done g_ht_done g_ht_ready gd_done g_y_ready")
        f_idx_ready, ft_done, f_hi_ready, f_lo_ready, fu_done, f_act_ready, f_h_ready, f_top_done, f_size_done, f_scale_done, f_h_hi_done, f_h_lo_done, f_ht_done, f_ht_ready, fd_done, f_c0_done, f_c1_done, f_c2_done, f_out_ready = sems(
            "f_idx_ready ft_done f_hi_ready f_lo_ready fu_done f_act_ready f_h_ready f_top_done f_size_done f_scale_done f_h_hi_done f_h_lo_done f_ht_done f_ht_ready fd_done f_c0_done f_c1_done f_c2_done f_out_ready")

        def tile(J, v, lag, deep=2, span=2):
            return span * J + (v - lag), span // deep * J + (v - lag) // deep, (v - lag) % deep

        def live(n, total):
            return not isinstance(n, int) or 0 <= n < total

        def need(eng, sem, value):
            if not isinstance(value, int) or value > 0:
                eng.wait_ge(sem, value)

        def hold(eng, passed_by, *waits):
            for sem, value in waits:
                need(eng, sem, value)
            if not all(isinstance(value, int) for _, value in waits):
                eng.sem_inc(passed_by, 1)

        def pipeline(eng, body, total, lag, span=2, beside=None, inside=None, head=0, start=0):
            head = max(head, lag + 2 + span - 1) // span

            def written_out(its):
                for it in its:
                    body(it // span, it % span)
                    if beside is not None:
                        beside(it)

            written_out(range(start, head * span))
            with eng.Fori(head, total // span) as J:
                for v in range(span):
                    body(J, v)
                    if inside is not None:
                        inside(J, v)
            written_out(range(total, total + lag))

        def group(n, k, of=EC):
            return n * of + k + 1

        RANK_AT = 64

        LAG1, LAG2, LAG3, SPAN2 = 8, 4, 4, 4
        HEAD1 = 12
        peak_order = [i for pair in zip(range(CHUNKS), range(CHUNKS, ALL_CHUNKS)) for i in pair] + list(range(DOWN_CHUNKS, CHUNKS))
        PEAK_AT, peak_counts = 2, [2, 2, 2, 2, 2, 1, 1, 1, 1]

        def found_at(it):
            k = it - PEAK_AT
            return peak_order[sum(peak_counts[:max(k, 0)]):sum(peak_counts[:max(k + 1, 0)])]

        SPLIT_J = HEAD1 // 2
        w_gu_flat = w_gu.rearrange("p x c n -> p (x c n)")
        s_gu_flat = s_gu.rearrange("p c n -> p (c n)")
        w_down_flat = w_down.rearrange("p x c n -> p (x c n)")

        def chunk_src(i):
            if i >= CHUNKS:
                return w_down_flat[:, (i - CHUNKS) * CH:(i - CHUNKS + 1) * CH]
            n = EXPERT_CHUNKS
            return w_gu_flat[:, i * CH:(i + 1) * CH] if i < n else s_gu_flat[:, (i - n) * CH:(i - n + 1) * CH]

        assert NT // 2 - SPLIT_J == CHUNKS

        block = ctx.enter_context(nc.Block())

        @block.sync
        def _(sp):
            sp.dma_start(wq_raw, wq_t.rearrange("p c n -> p (c n)")).then_inc(wq_in, 16)
            for dst, src in ((gate_raw[:, :], gates), (bq_s[:, :], bq), (bk_s[:, :], bk), (bv_s, bv),
                             (router_s[:, :, :], router), (pad_raw[:, :, :], pad)):
                sp.dma_start(dst, src).then_inc(small_in, 16)
            for dst, src in ((ctx_s, ctx_t), (wk_s, wk_t), (wv_s, wv_t)):
                sp.dma_start(dst, src).then_inc(kv_in, 16)

            def body(J, v):
                n, j, u = tile(J, v, 6)
                if live(n, NT):
                    sp.wait_ge(x1_ready, n + 1)
                    sp.dma_start(x1_dram[bass.ds(j * P + u * S, P), :], x1[u]).then_inc(x1_out[u], 16)
                n, j, u = tile(J, v, 7)
                if live(n, NT):
                    sp.wait_ge(xn2_ready, n + 1)
                    sp.dma_start(xn_dram[bass.ds(j * P + u * S, P), :], xn2[u]).then_inc(xn2_out[u], 16)
                n, j, u = tile(J, v, 0)
                if live(n, NT):
                    need(sp, xn_ready, n - 1)
                    sp.dma_start(x_in[u], x_tiles[bass.ds(j + u * HALF, 1)].rearrange("a p d -> (a p) d")).then_inc(x_here[u], 16)
                    if u == 0:
                        need(sp, sub_set, j)
                        sp.dma_start(sub_raw, sub_tiles[bass.ds(j, 1)].rearrange("a p d -> (a p) d")).then_inc(sub_here, 16)
                n, j, u = tile(J, v, 4)
                if live(n, NT):
                    need(sp, x1_ready, n - 1)
                    sp.dma_start(x_res[u], x_tiles[bass.ds(j + u * HALF, 1)].rearrange("a p d -> (a p) d")).then_inc(res_here[u], 16)

            def beside(it):
                if it == NT + 1:
                    sp.wait_ge(xt_done, NT)
                    sp.dma_start(last_raw, chunk_src(ALL_CHUNKS - 1)).then_inc(again_in[-1], 16)

            pipeline(sp, body, NT, LAG1, beside=beside, head=HEAD1)
            for u in range(2):
                sp.wait_ge(x1_out[u], 16 * HALF)
                sp.wait_ge(xn2_out[u], 16 * HALF)
                sp.wait_ge(rows_out[u], 16 * TOP * HALF)
            sp.wait_ge(plan_ready, 1)
            sp.drain().then_inc(pass1_over, 1)
            sp.wait_ge(pass1_over, 5)
            def body2(J, v):
                s, j, u = tile(J, v, 0, 4, SPAN2)
                if live(s, SLOTS):
                    need(sp, xg_here[u], 16 * j)
                    r = sp.value_load(slot_row[0:1, bass.ds(s, 1)], min_val=0, max_val=LISTS - P)
                    sp.dma_start(id_in[u], list_dram[bass.ds(r, P), :]).then_inc(id_here[u], 16)

            def body3(J, v):
                n, j, u = tile(J, v, 0)
                if live(n, NT):
                    need(sp, ft_done, n - 1)
                    sp.dma_start(f_x[u], xn_dram[bass.ds(j * P + u * S, P), :]).then_inc(f_x_here[u], 16)
                n, j, u = tile(J, v, 2)
                if live(n, NT):
                    need(sp, f_out_ready, n - 1)
                    sp.dma_start(f_x1[u], x1_dram[bass.ds(j * P + u * S, P), :]).then_inc(f_x1_here[u], 16)

            def beside2(it):
                if it == 3:
                    sp.dma_start(swd_raw, s_down.rearrange("p c n -> p (c n)")).then_inc(swd_in, 16)
                if it >= SLOTS:
                    body3((it - SLOTS) // 2, it % 2)

            pipeline(sp, body2, SLOTS, LAG2, SPAN2, beside=beside2)
            pipeline(sp, body3, NT, LAG3, start=LAG2)

        @block.gpsimd
        def _(pool):
            g = nc.gpsimd
            g.memset(ident[:, :], 0.0).then_inc(pool_set, 1)
            g.memset(ones[:, :], 1.0).then_inc(pool_set, 1)
            g.memset(half_power[:, :], -0.5).then_inc(pool_set, 1)
            g.memset(zeros_i[:, :], 0).then_inc(pool_set, 1)
            g.memset(seen[:, :], 0.0).then_inc(seen_zero, 1)
            pool.wait_ge(pool_set, 4)
            pool.dma_start(list_dram.rearrange("(p n) a -> p (n a)", p=P), zeros_i[:, :]).then_inc(list_zero, 16)
            g.affine_select(out=ident[:, :], in_=ident[:, :], compare_op=ALU.not_equal, fill=1.0, base=0,
                            pattern=[[-1, P]], channel_multiplier=1).then_inc(const_set, 1)
            g.affine_select(out=before[:, :], in_=ones[:, :], compare_op=ALU.is_gt, fill=0.0, base=0,
                            pattern=[[1, P]], channel_multiplier=-1).then_inc(const_set, 1)
            g.iota(expert_no[:, :], [[1, NX]], base=0, channel_multiplier=0, allow_small_or_imprecise_dtypes=True).then_inc(const_set, 1)
            g.iota(region_at[:, :], [[REGION, NX]], base=0, channel_multiplier=0, allow_small_or_imprecise_dtypes=True).then_inc(const_set, 1)
            g.iota(token_no[:, :, :], [[P, HALF], [S, B]], base=0, channel_multiplier=1).then_inc(const_set, 1)
            g.iota(step_at[:, :], [[P, NT]], base=0, channel_multiplier=0, allow_small_or_imprecise_dtypes=True).then_inc(const_set, 1)
            g.iota(slot_no[:, :], [[1, SLOTS]], base=0, channel_multiplier=0, allow_small_or_imprecise_dtypes=True).then_inc(const_set, 1)
            g.iota(upto_e[:, :, :], [[1, NX], [-1, NX]], base=0, channel_multiplier=0, allow_small_or_imprecise_dtypes=True).then_inc(const_set, 1)
            pool.wait_ge(small_in, 96)
            pool.wait_ge(const_set, 8)
            g.tensor_scalar(upto_e[:, :, :], upto_e[:, :, :], 0.0, None, ALU.is_ge).then_inc(const_set, 1)
            g.tensor_scalar(pad_bias[:, :, :], pad_raw[:, :, :], 0.0, MASKED, ALU.is_equal, ALU.mult).then_inc(const_set, 1)
            pool.wait_ge(const_set, 10)
            g.tensor_scalar(pad_keep[:, :, :], pad_bias[:, :, :], 0.0, None, ALU.is_equal).then_inc(const_set, 1)
            pool.wait_ge(peak_set, 1)
            g.partition_all_reduce(peak_all[:, 0:1], peak[:, 0:1], P, RMAX).then_inc(scale_set, 1)
            pool.wait_ge(const_set, 11)
            pool.wait_ge(list_zero, 16)

            def body(J, v):
                def shift(k):
                    n, j, u = tile(J, v, 3)
                    if live(n, NT):
                        pool.wait_ge(max_done, group(n, k))
                        sc = score[u].rearrange("p (h t) -> p h t", h=H)[:, k * HG:(k + 1) * HG, :]
                        mx = peaks_of[u][:, k * HG:(k + 1) * HG].unsqueeze(2).to_broadcast([P, HG, T])
                        g.tensor_tensor(sc, sc, mx, ALU.subtract).then_inc(shift_done, 1)

                shift(0)
                n, j, u = tile(J, v, 2)
                if live(n, NT):
                    if u == 0:
                        hold(pool, pool_passed, (sub_here, 16 * (j + 1)))
                        g.tensor_scalar(sub_bias, sub_raw, 0.0, MASKED, ALU.is_equal, ALU.mult).then_inc(sub_set, 1)
                    pool.wait_ge(sub_set, j + 1)
                    need(pool, max_done, group(n - 2, EC - 1))
                    g.tensor_tensor(mask_bias[u], sub_bias, pad_keep[:, u, :], ALU.mult).then_inc(mask_half, 1)
                shift(1)
                if live(n, NT):
                    pool.wait_ge(mask_half, n + 1)
                    g.tensor_tensor(mask_bias[u], mask_bias[u], pad_bias[:, u, :], ALU.add).then_inc(mask_set, 1)
                shift(2)
                n, j, u = tile(J, v, 5)
                if live(n, NT):
                    hold(pool, pool_passed, (ln2_mv, n + 1))
                    g.tensor_scalar(norm2[u][:, 0:1], mv2[u][:, 1:2], EPS, None, ALU.add).then_inc(ln2_eps, 1)
                    pool.wait_ge(ln2_eps, n + 1)
                    g.tensor_tensor(norm2[u][:, 1:2], norm2[u][:, 0:1], half_power[:, :], ALU.pow).then_inc(ln2_std, 1)
                n, j, u = tile(J, v, 0)
                if live(n, NT):
                    hold(pool, pool_passed, (ln1_mv, n + 1))
                    g.tensor_scalar(norm[u][:, 0:1], mv[u][:, 1:2], EPS, None, ALU.add).then_inc(ln1_eps, 1)
                    pool.wait_ge(ln1_eps, n + 1)
                    g.tensor_tensor(norm[u][:, 1:2], norm[u][:, 0:1], half_power[:, :], ALU.pow).then_inc(ln1_std, 1)
                    hold(pool, pool_passed, (ln1_std, n + 1))
                    g.tensor_scalar(norm[u][:, 2:3], mv[u][:, 0:1], norm[u][:, 1:2], -1.0, ALU.mult, ALU.mult).then_inc(ln1_norm, 1)
                n, j, u = tile(J, v, 8)
                if live(n, NT):
                    need(pool, rows_out[u], 16 * TOP * j)
                    g.tensor_copy(tok_i[u], token_no[:, :, :].rearrange("p j b -> p (j b)")[:, bass.ds(n, 1)]).then_inc(tok_ready, 1)
                    hold(pool, pool_passed, (tok_ready, n + 1), (row_ready, n + 1))
                    for k in range(TOP):
                        g.indirect_dma_start(list_dram, bass.IndirectOffsetOnAxis(ap=row_i[u][:, k:k + 1], axis=0),
                                             tok_i[u], None).then_inc(rows_out[u], 16)

            def beside(it):
                if it == CHUNKS:
                    pool.wait_ge(peak_set, 2)
                    g.partition_all_reduce(peak_all[:, 1:3], peak[:, 16:18], P, RMAX).then_inc(scale_set, 1)

            pipeline(pool, body, NT, LAG1, beside=beside, head=HEAD1)
            g.drain().then_inc(pass1_over, 1)
            pool.wait_ge(pass1_over, 5)

            def body2(J, v):
                s, j, u = tile(J, v, 0, 4, SPAN2)
                if live(s, SLOTS):
                    hold(pool, pool_passed, (gt_done, s - 3), (id_here[u], 16 * (j + 1)))
                    g.indirect_dma_start(xg[u], None, xn_dram, bass.IndirectOffsetOnAxis(ap=id_in[u], axis=0)).then_inc(xg_here[u], 16)

            def body3(J, v):
                n, j, u = tile(J, v, 1)
                if live(n, NT):
                    need(pool, f_y_here[u], 16 * TOP * j)
                    for k in range(TOP):
                        g.tensor_copy(f_idx[u][k], row_all[:, bass.ds(n * TOP + k, 1)]).then_inc(f_idx_ready, 1)
                    hold(pool, pool_passed, (f_idx_ready, n * TOP + TOP), (f_c2_done, n - 1))
                    for k in range(TOP):
                        g.indirect_dma_start(f_y[u][k], None, y_dram, bass.IndirectOffsetOnAxis(ap=f_idx[u][k], axis=0)).then_inc(f_y_here[u], 16)

            def beside2(it):
                if it == 2:
                    pool.wait_ge(peak_set, 3)
                    g.partition_all_reduce(peak_all[:, 3:4], peak[:, 18:19], P, RMAX).then_inc(scale_set, 1)
                if it == SLOTS + 1:
                    for u in range(2):
                        pool.wait_ge(y_out[u], 16 * SLOTS // 2)
                if it >= SLOTS:
                    body3((it - SLOTS) // 2, it % 2)

            pipeline(pool, body2, SLOTS, LAG2, SPAN2, beside=beside2)
            pipeline(pool, body3, NT, LAG3, start=LAG2)

        @block.scalar
        def _(act):
            a = nc.scalar
            act.wait_ge(small_in, 96)
            a.activation(gate[:, :], gate_raw[:, :], ACT.Tanh).then_inc(gate_set, 1)
            act.wait_ge(const_set, 1)
            a.activation(ident16[:, :], ident[:, :], ACT.Copy).then_inc(gate_set, 1)
            act.wait_ge(scale_set, 3)
            a.activation(wq[:, 0, :], wq_raw, ACT.Copy, scale=w_scale[:, 0:1]).then_inc(prep_hi, 1)

            def body(J, v):
                n, j, u = tile(J, v, 2)
                if live(n, NT):
                    act.wait_ge(xt_done, n + 1)
                    need(act, q_done, n)
                    a.activation(x_hi, bank[0][:, :], ACT.Copy, scale=X_SCALE).then_inc(hi_ready, 1)

                def take_probs(k):
                    n, j, u = tile(J, v, 4)
                    if live(n, NT):
                        act.wait_ge(pt_done, group(n, k))
                        need(act, av_done, group(n, k - 2))
                        a.activation(probs_t[k % 2], bank[4 + k % 2][:, :], ACT.Copy).then_inc(pt_ready, 1)

                def exponent(k):
                    n, j, u = tile(J, v, 3)
                    if live(n, NT):
                        act.wait_ge(shift_done, group(n, k, EC - 1))
                        sc = score[u][:, k * HG * T:(k + 1) * HG * T]
                        a.activation(sc, sc, ACT.Exp).then_inc(exp_done, 1)

                take_probs(0)
                take_probs(1)
                n, j, u = tile(J, v, 7)
                if live(n, NT):
                    act.wait_ge(logit_shift, n + 1)
                    need(act, r_idx_done, n)
                    a.activation(r_exp, bank[1][:, 0:NX], ACT.Exp, bias=logit_neg, accum_out=r_sum).then_inc(r_exp_done, 1)
                exponent(0)
                n, j, u = tile(J, v, 1)
                if live(n, NT):
                    act.wait_ge(ln1_norm, n + 1)
                    need(act, xt_done, n - 1)
                    a.activation(xn[u], x_in[u], ACT.Identity, scale=norm[u][:, 1:2], bias=norm[u][:, 2:3]).then_inc(xn_ready, 1)
                exponent(1)
                take_probs(2)
                take_probs(3)
                n, j, u = tile(J, v, 6)
                if live(n, NT):
                    act.wait_ge(x2t_done, n + 1)
                    need(act, logits_done, n)
                    a.activation(xn2_t, bank[1][:, :], ACT.Copy).then_inc(x2t_ready, 1)
                exponent(2)
                n, j, u = tile(J, v, 3)
                if live(n, NT):
                    act.wait_ge(neg_done, n + 1)
                    for h in range(H - HG, H):
                        sc = score[u][:, h * T:(h + 1) * T]
                        last = a.activation(sc, sc, ACT.Exp, bias=peaks_neg[:, h - H + HG:h - H + HG + 1])
                    last.then_inc(exp_done, 1)
                n, j, u = tile(J, v, 2)
                if live(n, NT):
                    act.wait_ge(q_done, n + 1)
                    need(act, s_done, group(n - 2, EC - 1))
                    for c in range(EC):
                        last = a.activation(q_t[u][:, c * P:(c + 1) * P], bank[0][:, c * P:(c + 1) * P], ACT.Identity,
                                            scale=w_back[:, 0:1], bias=bq_s[:, c:c + 1])
                    last.then_inc(q_ready, 1)

            def beside(it):
                for i in found_at(it + 2):
                    if i >= CHUNKS:
                        act.dma_start(weights[:, i * CH:(i + 1) * CH], chunk_src(i)).then_inc(chunk_in[i], 16)
                        continue
                    if i == CHUNKS - 1:
                        act.wait_ge(peak_step, 2 * DOWN_CHUNKS)
                    act.dma_start(raw(i), chunk_src(i)).then_inc(chunk_in[i], 16)
                if it == CHUNKS:
                    for i in range(CHUNKS, ALL_CHUNKS - 1):
                        act.dma_start(raw(i), chunk_src(i)).then_inc(again_in[i - CHUNKS], 16)
                if it == HEAD1 - 1:
                    act.wait_ge(scale_set, 8)
                if NT <= it < NT + DOWN_CHUNKS:
                    i = it - NT + CHUNKS
                    act.wait_ge(prep_lo, i + 1)
                    act.wait_ge(again_in[it - NT], 16)
                    src = raw(i) if i < ALL_CHUNKS - 1 else last_raw
                    a.activation(down_halves(i)[0], by_expert(src), ACT.Copy, scale=w_scale[:, 2:3]).then_inc(prep_hi, 1)

            def inside(J, v):
                if v != 0:
                    return
                i = J - SPLIT_J
                act.wait_ge(prep_lo, i + 1)
                a.activation(halves(i)[0], raw(i), ACT.Copy, scale=w_scale[:, 1:2]).then_inc(prep_hi, 1)

            pipeline(act, body, NT, LAG1, beside=beside, inside=inside, head=HEAD1)
            a.drain().then_inc(pass1_over, 1)
            act.wait_ge(pass1_over, 5)

            def body2(J, v):
                s, j, u = tile(J, v, 3, 2, SPAN2)
                if live(s, SLOTS):
                    act.wait_ge(g_ht_done, s + 1)
                    need(act, gd_done, s)
                    a.activation(g_ht, bank[5][:, :].bitcast(F16)[:, 0:2 * DX], ACT.Copy).then_inc(g_ht_ready, 1)
                s, j, u = tile(J, v, 4, 2, SPAN2)
                if live(s, SLOTS):
                    act.wait_ge(g_y_ready, s + 1)
                    act.dma_start(y_dram[bass.ds(s * P, P), :], g_y[u]).then_inc(y_out[u], 16)
                s, j, u = tile(J, v, 2, 2, SPAN2)
                if live(s, SLOTS):
                    act.wait_ge(g_scale_done, s + 1)
                    need(act, g_ht_done, s - 1)
                    a.activation(g_h_hi[u], g_h[u], ACT.Copy, scale=g_scale[u]).then_inc(g_h_hi_done, 1)
                s, j, u = tile(J, v, 0, 2, SPAN2)
                if live(s, SLOTS):
                    act.wait_ge(gt_done, s + 1)
                    need(act, gu_done, s - 1)
                    a.activation(g_hi[u], bank[u][:, :], ACT.Copy, scale=X_SCALE).then_inc(g_hi_ready, 1)
                s, j, u = tile(J, v, 1, 2, SPAN2)
                if live(s, SLOTS):
                    act.wait_ge(gu_done, s + 1)
                    need(act, g_h_ready, s - 1)
                    a.activation(g_act[u], bank[2 + u][:, 0:DX], ACT.Silu, scale=w_back[:, 1:2]).then_inc(g_act_ready, 1)

            def body3(J, v):
                n, j, u = tile(J, v, 3)
                if live(n, NT):
                    act.wait_ge(f_ht_done, n + 1)
                    need(act, fd_done, n)
                    a.activation(f_ht, bank[6][:, :].bitcast(F16), ACT.Copy).then_inc(f_ht_ready, 1)
                n, j, u = tile(J, v, 4)
                if live(n, NT):
                    act.wait_ge(f_out_ready, n + 1)
                    act.dma_start(out_tiles[bass.ds(j + u * HALF, 1)].rearrange("a p d -> (a p) d"), f_out[u]).then_inc(f_out_done[u], 16)
                n, j, u = tile(J, v, 2)
                if live(n, NT):
                    act.wait_ge(f_scale_done, n + 1)
                    need(act, f_ht_done, n - 1)
                    a.activation(f_h_hi[u], f_h[u], ACT.Copy, scale=f_scale[u]).then_inc(f_h_hi_done, 1)
                n, j, u = tile(J, v, 0)
                if live(n, NT):
                    act.wait_ge(ft_done, n + 1)
                    need(act, fu_done, n - 1)
                    a.activation(f_hi[u], bank[u][:, :], ACT.Copy, scale=X_SCALE).then_inc(f_hi_ready, 1)
                n, j, u = tile(J, v, 1)
                if live(n, NT):
                    act.wait_ge(fu_done, n + 1)
                    need(act, f_h_ready, n - 1)
                    a.activation(f_act[u], bank[2 + u][:, :], ACT.Silu, scale=w_back[:, 1:2]).then_inc(f_act_ready, 1)

            def beside2(it):
                if it == 4:
                    act.wait_ge(scale_set, 11)
                    a.activation(swd[:, 0, :], swd_raw, ACT.Copy, scale=w_scale[:, 3:4]).then_inc(prep_hi, 1)
                if it >= SLOTS:
                    body3((it - SLOTS) // 2, it % 2)

            pipeline(act, body2, SLOTS, LAG2, SPAN2, beside=beside2)
            pipeline(act, body3, NT, LAG3, start=LAG2)
            for u in range(2):
                act.wait_ge(f_out_done[u], 16 * HALF)

        @block.vector
        def _(dve):
            d = nc.vector
            d.memset(kbd, 0.0).then_inc(kv_set, 1)
            d.memset(vaug[:, :, :, D:D + 1], 1.0)
            dve.wait_ge(wq_in, 16)
            d.tensor_reduce(peak[:, 0:1], wq_raw, AX.X, ALU.max, apply_absolute_value=True).then_inc(peak_set, 1)

            def scale_of(i, at):
                dve.wait_ge(scale_set, at)
                d.tensor_scalar(w_back[:, i:i + 1], peak_all[:, i:i + 1], TINY, None, ALU.max).then_inc(scale_set, 1)
                dve.wait_ge(scale_set, at + 1)
                bits = w_back[:, i:i + 1].bitcast(I32)
                d.tensor_scalar(bits, bits, EXPONENT, None, ALU.bitwise_and).then_inc(scale_step, 1)
                dve.wait_ge(scale_step, 1 + 2 * i)
                d.reciprocal(w_scale[:, i:i + 1], w_back[:, i:i + 1]).then_inc(scale_step, 1)
                dve.wait_ge(scale_step, 2 + 2 * i)
                back = 1.0 / W_TOP if i >= 2 else 1.0 / (W_TOP * X_SCALE)
                d.tensor_scalar(w_back[:, i:i + 1], w_back[:, i:i + 1], back, None, ALU.mult)
                d.tensor_scalar(w_scale[:, i:i + 1], w_scale[:, i:i + 1], W_TOP, None, ALU.mult).then_inc(scale_set, 1)
                dve.wait_ge(scale_set, at + 2)

            scale_of(0, 1)
            dve.wait_ge(prep_hi, 1)
            d.scalar_tensor_tensor(wq[:, 1, :], wq_raw, w_scale[:, 0:1], wq[:, 0, :], ALU.mult, ALU.subtract).then_inc(prep_lo, 1)
            def keys_and_values():
                dve.wait_ge(small_in, 96)
                dve.wait_ge(kv_set, 1)
                for c in range(EC):
                    dve.wait_ge(kv_mm, 1)
                    for b in range(B):
                        for h in range(HG):
                            rows = slice(h * D, (h + 1) * D)
                            d.tensor_scalar(kbd[rows, b, c, h * T:(h + 1) * T], bank[c][rows, b * T:(b + 1) * T],
                                            bk_s[rows, c:c + 1], float(D) ** -0.5, ALU.add, ALU.mult)
                dve.wait_ge(kv_mm, 2)
                for b in range(B):
                    last = d.tensor_tensor(vaug[:, b, :, 0:D], bank[4 + b][:, :].rearrange("p (h d) -> p h d", h=H),
                                           bv_s.rearrange("p (h d) -> p h d", h=H), ALU.add)
                last.then_inc(kv_set, 1)

            dve.wait_ge(gate_set, 2)
            dve.wait_ge(const_set, 11)
            dve.wait_ge(seen_zero, 1)

            def body(J, v):
                def maxima(k):
                    n, j, u = tile(J, v, 3)
                    if live(n, NT):
                        hold(dve, dve_passed, (s_done, group(n, k)), (mask_set, n + 1), (pt_done, group(n - 2, k)))
                        for h in range(HG):
                            hh = k * HG + h
                            last = d.tensor_tensor_reduce(score[u][:, hh * T:(hh + 1) * T], bank[2 + k % 2][:, h * T:(h + 1) * T],
                                                          mask_bias[u], 1.0, LOWEST, ALU.add, ALU.max, peaks_of[u][:, hh:hh + 1])
                        last.then_inc(max_done, 1)

                hs = H // 2

                def normalise(half, lag):
                    n, j, u = tile(J, v, lag)
                    if live(n, NT):
                        av = bank[6 + half][:, 0:hs * (D + 1)].rearrange("p (h d) -> p h d", h=hs)
                        inv = inv_sum[:, half * hs:(half + 1) * hs]
                        dve.wait_ge(av_done, group(n, 2 * half + 1))
                        d.reciprocal(inv, av[:, :, D]).then_inc(inv_done[half], 1)
                        dve.wait_ge(inv_done[half], n + 1)
                        d.tensor_tensor(attn[:, half * hs * D:(half + 1) * hs * D].rearrange("p (h d) -> p h d", h=hs), av[:, :, 0:D],
                                        inv.unsqueeze(2).to_broadcast([P, hs, D]), ALU.mult).then_inc(attn_done[half], 1)

                n0, j0, u0 = tile(J, v, 0)
                n5, j5, u5 = tile(J, v, 5)
                n7, j7, u7 = tile(J, v, 7)
                n8, j8, u8 = tile(J, v, 8)
                n, j, u = tile(J, v, 6)
                if live(n, NT):
                    dve.wait_ge(ln2_std, n + 1)
                    need(dve, x2t_done, n - 1)
                    need(dve, xn2_out[u], 16 * j)
                    d.tensor_scalar(xn2[u], x1[u], mv2[u][:, 0:1], norm2[u][:, 1:2], ALU.subtract, ALU.mult).then_inc(xn2_ready, 1)
                n, j, u = tile(J, v, 2)
                if live(n, NT):
                    dve.wait_ge(hi_ready, n + 1)
                    d.scalar_tensor_tensor(x_lo, bank[0][:, :], X_SCALE, x_hi, ALU.mult, ALU.subtract).then_inc(lo_ready, 1)
                if live(n8, NT):
                    dve.wait_ge(rank_done, n8 + 1)
                    if live(n7, NT):
                        dve.wait_ge(logits_done, n7 + 1)
                    d.tensor_tensor(at_row, bank[1][:, RANK_AT:RANK_AT + NX], region_at[:, :], ALU.add).then_inc(at_row_done, 1)
                    d.tensor_tensor(seen[:, :], seen[:, :], chosen[u8], ALU.add).then_inc(seen_done, 1)
                if live(n7, NT):
                    dve.wait_ge(logits_done, n7 + 1)
                    d.tensor_reduce(logit_neg, bank[1][:, 0:NX], AX.X, ALU.max, negate=True).then_inc(logit_shift, 1)
                maxima(0)
                maxima(1)
                normalise(1, 5)
                if live(n5, NT):
                    dve.wait_ge(res_here[u5], 16 * (j5 + 1))
                    dve.wait_ge(attn_done[0], n5 + 1)
                    dve.wait_ge(attn_done[1], n5 + 1)
                    need(dve, x1_out[u5], 16 * j5)
                    d.scalar_tensor_tensor(x1[u5], attn, gate[:, 0:1], x_res[u5], ALU.mult, ALU.add).then_inc(x1_ready, 1)
                maxima(2)
                if live(n5, NT):
                    dve.wait_ge(x1_ready, n5 + 1)
                    d.bn_stats(stats2[u5], x1[u5]).then_inc(ln2_stats, 1)
                maxima(EC - 1)
                if live(n7, NT):
                    hold(dve, dve_passed, (r_exp_done, n7 + 1))
                    d.max(r_top, r_exp).then_inc(r_top_done, 1)
                    d.reciprocal(r_inv, r_sum).then_inc(r_inv_done, 1)
                n, j, u = tile(J, v, 3)
                if live(n, NT):
                    dve.wait_ge(max_done, group(n, EC - 1))
                    need(dve, exp_done, group(n - 1, EC - 1))
                    d.tensor_scalar(peaks_neg, peaks_of[u][:, H - HG:H], -1.0, None, ALU.mult).then_inc(neg_done, 1)
                if live(n5, NT):
                    hold(dve, dve_passed, (ln2_stats, n5 + 1))
                    d.bn_aggr(mv2[u5], stats2[u5]).then_inc(ln2_mv, 1)
                if live(n7, NT):
                    hold(dve, dve_passed, (r_top_done, n7 + 1))
                    d.max_index(r_idx, r_top, r_exp).then_inc(r_idx_done, 1)
                if live(n8, NT):
                    dve.wait_ge(at_row_done, n8 + 1)
                    d.tensor_tensor_reduce(junk[0], at_row, first[u8], 1.0, 0.0, ALU.mult, ALU.add, row_f[:, 0:1])
                    d.tensor_tensor_reduce(junk[1], at_row, second[u8], 1.0, 0.0, ALU.mult, ALU.add, row_f[:, 1:2]).then_inc(row_f_done, 1)
                if live(n7, NT):
                    dve.wait_ge(r_idx_done, n7 + 1)
                    d.tensor_scalar(first[u7], expert_no[:, :], r_idx[:, 0:1], None, ALU.is_equal)
                    d.tensor_scalar(second[u7], expert_no[:, :], r_idx[:, 1:2], None, ALU.is_equal).then_inc(first_done, 1)
                    dve.wait_ge(r_inv_done, n7 + 1)
                    d.tensor_scalar(prob_all[:, bass.ds(n7 * TOP, TOP)], r_top[:, 0:TOP], r_inv, None, ALU.mult)
                    dve.wait_ge(first_done, n7 + 1)
                    d.tensor_tensor(chosen[u7], first[u7], second[u7], ALU.add).then_inc(chosen_done, 1)
                if live(n0, NT):
                    dve.wait_ge(x_here[u0], 16 * (j0 + 1))
                    d.bn_stats(stats[u0], x_in[u0]).then_inc(ln1_stats, 1)
                if live(n8, NT):
                    dve.wait_ge(row_f_done, n8 + 1)
                    need(dve, rows_out[u8], 16 * TOP * j8)
                    d.tensor_copy(row_i[u8], row_f).then_inc(row_ready, 1)
                    d.tensor_copy(row_list[:, bass.ds(n8 * TOP, TOP)], row_f)
                if live(n0, NT):
                    hold(dve, dve_passed, (ln1_stats, n0 + 1))
                    d.bn_aggr(mv[u0], stats[u0]).then_inc(ln1_mv, 1)
                normalise(0, 4)

            def beside(it):
                def largest(i, w):
                    dve.wait_ge(chunk_in[i], 16)
                    d.tensor_reduce(peak[:, 1 + i:2 + i], w, AX.X, ALU.max, apply_absolute_value=True).then_inc(peak_step, 1)

                if it == 1:
                    keys_and_values()
                for i in found_at(it):
                    largest(i, raw(i) if i < CHUNKS else weights[:, i * CH:(i + 1) * CH])
                if it == PEAK_AT + len(peak_counts) - 1:
                    dve.wait_ge(peak_step, ALL_CHUNKS)
                    d.tensor_reduce(peak[:, 16:17], peak[:, 1:1 + CHUNKS], AX.X, ALU.max)
                    d.tensor_reduce(peak[:, 17:18], peak[:, 1 + CHUNKS:1 + ALL_CHUNKS], AX.X, ALU.max).then_inc(peak_set, 1)
                if it == HEAD1 - 1:
                    scale_of(1, 4)
                    scale_of(2, 6)
                if NT <= it < NT + DOWN_CHUNKS:
                    i = it - NT + CHUNKS
                    hi, lo = down_halves(i)
                    src = raw(i) if i < ALL_CHUNKS - 1 else last_raw
                    dve.wait_ge(prep_hi, i + 2)
                    d.scalar_tensor_tensor(lo, by_expert(src), w_scale[:, 2:3], hi, ALU.mult, ALU.subtract).then_inc(prep_lo, 1)

            def inside(J, v):
                if v != 1:
                    return
                i = J - SPLIT_J
                hi, lo = halves(i)
                dve.wait_ge(prep_hi, i + 2)
                d.scalar_tensor_tensor(lo, raw(i), w_scale[:, 1:2], hi, ALU.mult, ALU.subtract).then_inc(prep_lo, 1)

            pipeline(dve, body, NT, LAG1, beside=beside, inside=inside, head=HEAD1)
            d.drain().then_inc(pass1_over, 1)

            steps = [0]

            def link(ins):
                steps[0] += 1
                ins.then_inc(plan_step, 1)
                dve.wait_ge(plan_step, steps[0])

            dve.wait_ge(counts_done, 1)
            le = below.rearrange("p (e f) -> p e f", e=NX)
            r3 = reached.rearrange("p (e t) -> p e t", e=NX)
            link(d.tensor_tensor(r3, bank[0][:, 0:NX].unsqueeze(2).to_broadcast([P, NX, NT]),
                                 step_at[:, :].unsqueeze(1).to_broadcast([P, NX, NT]), ALU.is_gt))
            link(d.tensor_reduce(n_tiles, r3, AX.X, ALU.add))
            d.tensor_scalar(ahead, n_tiles, -float(P), float(REGION), ALU.mult, ALU.add)
            link(d.tensor_tensor(le, upto_e[:, :, :], n_tiles.unsqueeze(1).to_broadcast([P, NX, NX]), ALU.mult))
            link(d.tensor_reduce(upto, le, AX.X, ALU.add))
            p3 = passed.rearrange("p (s e) -> p s e", s=SLOTS)
            pn = passed_n.rearrange("p (s e) -> p s e", s=SLOTS)
            link(d.tensor_tensor(p3, slot_no[:, :].unsqueeze(2).to_broadcast([P, SLOTS, NX]),
                                 upto.unsqueeze(1).to_broadcast([P, SLOTS, NX]), ALU.is_ge))
            link(d.tensor_tensor(pn, p3, ahead.unsqueeze(1).to_broadcast([P, SLOTS, NX]), ALU.mult))
            link(d.tensor_reduce(row_sf, pn, AX.X, ALU.add))
            link(d.scalar_tensor_tensor(row_sf, slot_no[:, :], float(P), row_sf, ALU.mult, ALU.add))
            d.tensor_copy(slot_row[:, :], row_sf).then_inc(plan_ready, 1)
            link(d.tensor_reduce(expert_f, p3, AX.X, ALU.add))
            link(d.tensor_scalar(expert_f, expert_f, float(NX - 1), None, ALU.min))
            d.tensor_copy(slot_expert[:, :], expert_f).then_inc(plan_ready, 1)
            l3 = later.rearrange("p (r e) -> p r e", e=NX - 1)
            link(d.tensor_tensor(l3, row_list[:, :].unsqueeze(2).to_broadcast([P, NT * TOP, NX - 1]),
                                 region_at[:, 1:NX].unsqueeze(1).to_broadcast([P, NT * TOP, NX - 1]), ALU.is_ge))
            link(d.tensor_tensor(l3, l3, ahead[:, 0:NX - 1].unsqueeze(1).to_broadcast([P, NT * TOP, NX - 1]), ALU.mult))
            link(d.tensor_reduce(row_slots, l3, AX.X, ALU.add))
            link(d.tensor_tensor(row_slots, row_list[:, :], row_slots, ALU.subtract))
            link(d.tensor_copy(row_all[:, :], row_slots))
            dve.wait_ge(pass1_over, 5)

            def body2(J, v):
                s, j, u = tile(J, v, 2, 2, SPAN2)
                if live(s, SLOTS):
                    dve.wait_ge(g_h_hi_done, s + 1)
                    need(dve, g_ht_done, s - 1)
                    d.scalar_tensor_tensor(g_h_lo[u], g_h[u], g_scale[u], g_h_hi[u], ALU.mult, ALU.subtract).then_inc(g_h_lo_done, 1)
                s, j, u = tile(J, v, 0, 2, SPAN2)
                if live(s, SLOTS):
                    dve.wait_ge(g_hi_ready, s + 1)
                    need(dve, gu_done, s - 1)
                    d.scalar_tensor_tensor(g_lo[u], bank[u][:, :], X_SCALE, g_hi[u], ALU.mult, ALU.subtract).then_inc(g_lo_ready, 1)
                s, j, u = tile(J, v, 3, 2, SPAN2)
                size = g_size[(v - 3) % 4]
                if live(s, SLOTS):
                    dve.wait_ge(gd_done, s + 1)
                    need(dve, y_out[u], 16 * j)
                    d.tensor_scalar(g_y[u], bank[6 + u][:, :], size, w_back[:, 2:3], ALU.mult, ALU.mult).then_inc(g_y_ready, 1)
                s, j, u = tile(J, v, 1, 2, SPAN2)
                size = g_size[(v - 1) % 4]
                if live(s, SLOTS):
                    dve.wait_ge(g_act_ready, s + 1)
                    need(dve, g_h_lo_done, s - 1)
                    d.scalar_tensor_tensor(g_h[u], bank[2 + u][:, DX:2 * DX], w_back[:, 1:2], g_act[u], ALU.mult, ALU.mult).then_inc(g_h_ready, 1)
                    dve.wait_ge(g_h_ready, s + 1)
                    d.tensor_reduce(g_top, g_h[u], AX.X, ALU.max, apply_absolute_value=True).then_inc(g_top_done, 1)
                    dve.wait_ge(g_top_done, s + 1)
                    d.tensor_scalar(size, g_top, TINY, 1.0 / H_TOP, ALU.max, ALU.mult).then_inc(g_size_done, 1)
                    dve.wait_ge(g_size_done, s + 1)
                    d.reciprocal(g_scale[u], size).then_inc(g_scale_done, 1)

            def body3(J, v):
                n, j, u = tile(J, v, 2)
                if live(n, NT):
                    dve.wait_ge(f_h_hi_done, n + 1)
                    need(dve, f_ht_done, n - 1)
                    d.scalar_tensor_tensor(f_h_lo[u], f_h[u], f_scale[u], f_h_hi[u], ALU.mult, ALU.subtract).then_inc(f_h_lo_done, 1)
                n, j, u = tile(J, v, 0)
                if live(n, NT):
                    dve.wait_ge(f_hi_ready, n + 1)
                    need(dve, fu_done, n - 1)
                    d.scalar_tensor_tensor(f_lo[u], bank[u][:, :], X_SCALE, f_hi[u], ALU.mult, ALU.subtract).then_inc(f_lo_ready, 1)
                n, j, u = tile(J, v, 3)
                if live(n, NT):
                    dve.wait_ge(f_y_here[u], 16 * TOP * (j + 1))
                    d.tensor_scalar(f_c0, f_y[u][0], prob_all[:, bass.ds(n * TOP, 1)], None, ALU.mult).then_inc(f_c0_done, 1)
                    dve.wait_ge(fd_done, n + 1)
                    dve.wait_ge(f_c0_done, n + 1)
                    d.scalar_tensor_tensor(f_c1, bank[7][:, :], f_back[u], f_c0, ALU.mult, ALU.add).then_inc(f_c1_done, 1)
                    dve.wait_ge(f_c1_done, n + 1)
                    d.scalar_tensor_tensor(f_c2, f_y[u][1], prob_all[:, bass.ds(n * TOP + 1, 1)], f_c1, ALU.mult, ALU.add).then_inc(f_c2_done, 1)
                    dve.wait_ge(f_c2_done, n + 1)
                    dve.wait_ge(f_x1_here[u], 16 * (j + 1))
                    need(dve, f_out_done[u], 16 * j)
                    d.scalar_tensor_tensor(f_out[u], f_c2, gate[:, 1:2], f_x1[u], ALU.mult, ALU.add).then_inc(f_out_ready, 1)
                n, j, u = tile(J, v, 1)
                if live(n, NT):
                    dve.wait_ge(f_act_ready, n + 1)
                    need(dve, f_h_lo_done, n - 1)
                    d.scalar_tensor_tensor(f_h[u], bank[4 + u][:, :], w_back[:, 1:2], f_act[u], ALU.mult, ALU.mult).then_inc(f_h_ready, 1)
                    dve.wait_ge(f_h_ready, n + 1)
                    d.tensor_reduce(f_top, f_h[u], AX.X, ALU.max, apply_absolute_value=True).then_inc(f_top_done, 1)
                    dve.wait_ge(f_top_done, n + 1)
                    d.tensor_scalar(f_size[u], f_top, TINY, 1.0 / H_TOP, ALU.max, ALU.mult).then_inc(f_size_done, 1)
                    dve.wait_ge(f_size_done, n + 1)
                    d.tensor_scalar(f_back[u], f_size[u], w_back[:, 3:4], None, ALU.mult)
                    d.reciprocal(f_scale[u], f_size[u]).then_inc(f_scale_done, 1)

            def beside2(it):
                if it == 1:
                    dve.wait_ge(swd_in, 16)
                    d.tensor_reduce(peak[:, 18:19], swd_raw, AX.X, ALU.max, apply_absolute_value=True).then_inc(peak_set, 1)
                if it == 3:
                    scale_of(3, 9)
                if it == 5:
                    dve.wait_ge(prep_hi, 2 + ALL_CHUNKS)
                    d.scalar_tensor_tensor(swd[:, 1, :], swd_raw, w_scale[:, 3:4], swd[:, 0, :], ALU.mult, ALU.subtract).then_inc(prep_lo, 1)
                if it >= SLOTS:
                    body3((it - SLOTS) // 2, it % 2)

            pipeline(dve, body2, SLOTS, LAG2, SPAN2, beside=beside2)
            pipeline(dve, body3, NT, LAG3, start=LAG2)

        @block.tensor
        def _(pe):
            t = nc.tensor

            def transposes(dst, src, count):
                for c in range(count):
                    last = t.transpose(dst[:, c * P:(c + 1) * P], src[:, c * P:(c + 1) * P],
                                       (ident16 if src.dtype == F16 else ident)[:, :])
                return last

            def split_product(dst, hi, lo, w_hi, w_lo, chunks=EC):
                for c in range(chunks):
                    rows = slice(c * P, (c + 1) * P)
                    t.matmul(dst, hi[:, rows], w_hi(c), start=(c == 0), stop=False)
                    t.matmul(dst, hi[:, rows], w_lo(c), start=False, stop=False)
                    last = t.matmul(dst, lo[:, rows], w_hi(c), start=False, stop=(c == chunks - 1))
                return last

            pe.wait_ge(kv_in, 48)
            for co in range(EC):
                for ci in range(EC):
                    last = t.matmul(bank[co][:, 0:B * T], wk_s[:, ci, co * P:(co + 1) * P], ctx_s[:, ci, :],
                                    start=(ci == 0), stop=(ci == EC - 1))
            last.then_inc(kv_mm, 1)
            for b in range(B):
                for ci in range(EC):
                    last = t.matmul(bank[4 + b][:, :], ctx_s[:, ci, b * T:(b + 1) * T], wv_s[:, ci, :],
                                    start=(ci == 0), stop=(ci == EC - 1))
            last.then_inc(kv_mm, 1)
            pe.wait_ge(const_set, 11)
            pe.wait_ge(kv_set, 2)
            pe.wait_ge(prep_lo, 1)

            def body(J, v):
                n, j, u = tile(J, v, 2)
                if live(n, NT):
                    pe.wait_ge(xn_ready, n + 1)
                    need(pe, q_ready, n)
                    transposes(bank[0], xn[u], EC).then_inc(xt_done, 1)

                def scores(k):
                    n, j, u = tile(J, v, 3)
                    if live(n, NT):
                        pe.wait_ge(q_ready, n + 1)
                        need(pe, max_done, group(n, k - 2))
                        t.matmul(bank[2 + k % 2][:, :], q_t[u][:, k * P:(k + 1) * P], kbd[:, u, k, :],
                                 start=True, stop=True).then_inc(s_done, 1)

                def turn_probs(k):
                    n, j, u = tile(J, v, 4)
                    if live(n, NT):
                        pe.wait_ge(exp_done, group(n, k))
                        need(pe, pt_ready, group(n, k - 2))
                        transposes(bank[4 + k % 2], score[u][:, k * HG * T:(k + 1) * HG * T], HG).then_inc(pt_done, 1)

                def mix_values(k):
                    n, j, u = tile(J, v, 4)
                    if live(n, NT):
                        pe.wait_ge(pt_ready, group(n, k))
                        half = k // 2
                        need(pe, attn_done[half], n)
                        for h in range(HG):
                            at = (k % 2 * HG + h) * (D + 1)
                            last = t.matmul(bank[6 + half][:, at:at + D + 1], probs_t[k % 2][:, h * P:(h + 1) * P],
                                            vaug[:, u, k * HG + h, :], start=True, stop=True)
                        last.then_inc(av_done, 1)

                def queries(chunks):
                    n, j, u = tile(J, v, 2)
                    if live(n, NT):
                        pe.wait_ge(lo_ready, n + 1)
                        for co in chunks:
                            dst = bank[0][:, co * P:(co + 1) * P]
                            for ci in range(EC):
                                at = ci * E + co * P
                                xs = slice(ci * P, (ci + 1) * P)
                                t.matmul(dst, wq[:, 0, at:at + P], x_hi[:, xs], start=(ci == 0), stop=False)
                                t.matmul(dst, wq[:, 0, at:at + P], x_lo[:, xs], start=False, stop=False)
                                last = t.matmul(dst, wq[:, 1, at:at + P], x_hi[:, xs], start=False, stop=(ci == EC - 1))
                        if chunks[-1] == EC - 1:
                            last.then_inc(q_done, 1)

                turn_probs(0)
                turn_probs(1)
                scores(0)
                scores(1)
                mix_values(0)
                scores(2)
                mix_values(1)
                scores(3)
                turn_probs(2)
                turn_probs(3)
                n, j, u = tile(J, v, 6)
                if live(n, NT):
                    pe.wait_ge(xn2_ready, n + 1)
                    need(pe, r_exp_done, n)
                    need(pe, at_row_done, n - 1)
                    transposes(bank[1], xn2[u], EC).then_inc(x2t_done, 1)
                queries((0, 1))
                mix_values(2)
                queries((2, 3))
                mix_values(3)
                n6, j6, u6 = tile(J, v, 6)
                if live(n6, NT):
                    pe.wait_ge(x2t_ready, n6 + 1)
                n, j, u = tile(J, v, 7)
                if live(n, NT):
                    pe.wait_ge(chosen_done, n + 1)
                    need(pe, seen_done, n)
                    ranks = bank[1][:, RANK_AT:RANK_AT + NX]
                    t.matmul(ranks, before[:, :], chosen[u], start=True, stop=False)
                    t.matmul(ranks, ones[:, :], seen[:, :], start=False, stop=True).then_inc(rank_done, 1)
                if live(n6, NT):
                    for c in range(EC):
                        last = t.matmul(bank[1][:, 0:NX], xn2_t[:, c * P:(c + 1) * P], router_s[:, c, :],
                                        start=(c == 0), stop=(c == EC - 1))
                    last.then_inc(logits_done, 1)

            pipeline(pe, body, NT, LAG1, head=HEAD1)
            pe.wait_ge(seen_done, NT)
            pe.wait_ge(q_ready, NT)
            t.matmul(bank[0][:, 0:NX], ones[:, :], seen[:, :], start=True, stop=True).then_inc(counts_done, 1)
            t.drain().then_inc(pass1_over, 1)
            pe.wait_ge(pass1_over, 5)
            pe.wait_ge(prep_lo, 1 + ALL_CHUNKS)
            pe.wait_ge(plan_ready, 2)

            def body2(J, v):
                s, j, u = tile(J, v, 3, 2, SPAN2)
                if live(s, SLOTS):
                    pe.wait_ge(g_h_lo_done, s + 1)
                    need(pe, g_ht_ready, s)
                    dst = bank[5][:, :].bitcast(F16)
                    transposes(dst[:, 0:DX], g_h_hi[u], DX // P)
                    transposes(dst[:, DX:2 * DX], g_h_lo[u], DX // P).then_inc(g_ht_done, 1)
                s, j, u = tile(J, v, 0, 4, SPAN2)
                if live(s, SLOTS):
                    pe.wait_ge(xg_here[u], 16 * (j + 1))
                    need(pe, g_lo_ready, s - 1)
                    transposes(bank[u % 2], xg[u], EC).then_inc(gt_done, 1)
                s, j, u = tile(J, v, 1, 2, SPAN2)
                if live(s, SLOTS):
                    e = pe.value_load(slot_expert[0:1, bass.ds(s, 1)], min_val=0, max_val=NX - 1)
                    pe.wait_ge(g_lo_ready, s + 1)
                    need(pe, g_h_ready, s - 1)
                    w = 2 * DX
                    split_product(bank[2 + u][:, :], g_hi[u], g_lo[u],
                                  lambda c: gu[:, bass.ds(e * (2 * CH) + c * w, w)],
                                  lambda c: gu[:, bass.ds(e * (2 * CH) + (CH + c * w), w)]).then_inc(gu_done, 1)
                s, j, u = tile(J, v, 3, 2, SPAN2)
                if live(s, SLOTS):
                    e = pe.value_load(slot_expert[0:1, bass.ds(s, 1)], min_val=0, max_val=NX - 1)
                    pe.wait_ge(g_ht_ready, s + 1)
                    need(pe, g_y_ready, s - 1)
                    split_product(bank[6 + u][:, :], g_ht[:, 0:DX], g_ht[:, DX:2 * DX],
                                  lambda c: gu[:, bass.ds(e * (2 * XD) + (DOWN_AT + c * E), E)],
                                  lambda c: gu[:, bass.ds(e * (2 * XD) + (DOWN_AT + XD + c * E), E)], DX // P).then_inc(gd_done, 1)


            def shared(c, part, half):
                at = (2 * c + part) * DS
                return gu[:, bass.ds((2 * (EXPERT_CHUNKS + at // CH) + half) * CH + at % CH, DS)]

            def body3(J, v):
                n, j, u = tile(J, v, 3)
                if live(n, NT):
                    pe.wait_ge(f_h_lo_done, n + 1)
                    need(pe, f_ht_ready, n)
                    dst = bank[6][:, :].bitcast(F16)
                    transposes(dst[:, 0:DS], f_h_hi[u], DS // P)
                    transposes(dst[:, DS:2 * DS], f_h_lo[u], DS // P).then_inc(f_ht_done, 1)
                n, j, u = tile(J, v, 0)
                if live(n, NT):
                    pe.wait_ge(f_x_here[u], 16 * (j + 1))
                    need(pe, f_lo_ready, n - 1)
                    transposes(bank[u], f_x[u], EC).then_inc(ft_done, 1)
                n, j, u = tile(J, v, 1)
                if live(n, NT):
                    pe.wait_ge(f_lo_ready, n + 1)
                    need(pe, f_h_ready, n - 1)
                    for part in range(2):
                        last = split_product(bank[2 + 2 * part + u][:, :], f_hi[u], f_lo[u],
                                             lambda c: shared(c, part, 0), lambda c: shared(c, part, 1))
                    last.then_inc(fu_done, 1)
                n, j, u = tile(J, v, 3)
                if live(n, NT):
                    pe.wait_ge(f_ht_ready, n + 1)
                    need(pe, f_c1_done, n)
                    split_product(bank[7][:, :], f_ht[:, 0:DS], f_ht[:, DS:2 * DS],
                                  lambda c: swd[:, 0, c * E:(c + 1) * E], lambda c: swd[:, 1, c * E:(c + 1) * E], DS // P).then_inc(fd_done, 1)

            def beside2(it):
                if it == SLOTS:
                    pe.wait_ge(g_lo_ready, SLOTS)
                if it == SLOTS + 1:
                    pe.wait_ge(g_h_ready, SLOTS)
                if it == SLOTS + 2:
                    pe.wait_ge(g_ht_ready, SLOTS)
                if it == SLOTS + 3:
                    pe.wait_ge(g_y_ready, SLOTS)
                    pe.wait_ge(prep_lo, 2 + ALL_CHUNKS)
                if it >= SLOTS:
                    body3((it - SLOTS) // 2, it % 2)

            pipeline(pe, body2, SLOTS, LAG2, SPAN2, beside=beside2)
            pipeline(pe, body3, NT, LAG3, start=LAG2)


def kernel(**inputs):
    import concourse.bacc as bacc
    from concourse.bass_utils import run_bass_kernel_spmd

    got = {k: np.asarray(v) for k, v in inputs.items()}

    def rows(w, *lead):
        w = w.reshape(*w.shape[:-2], w.shape[-2] // P, P, w.shape[-1])
        return np.ascontiguousarray(np.moveaxis(w, -2, 0))

    def cols(b):
        return np.ascontiguousarray(b.reshape(EC, P).T)

    gate_up = np.concatenate([got["L0_ffn_experts_gate"], got["L0_ffn_experts_up"]], axis=-1)
    shared_gate_up = np.concatenate([got["L0_ffn_shared_gate"], got["L0_ffn_shared_up"]], axis=-1)
    arrays = {
        "x": got["x"],
        "ctx_t": rows(got["ctx_1024"].reshape(B * T, E).T),
        "pad": np.broadcast_to(got["mask_Bx1x1xS2_ik0"].reshape(1, B, T), (P, B, T)),
        "sub": got["mask_1x1xSxS2_ik0"],
        "gates": np.broadcast_to(np.concatenate([got["g_xattn"], got["g_ffn"]]).reshape(1, 2), (P, 2)),
        "wq_t": rows(got["L0_xattn_Wq"].T),
        "wk_t": rows(got["L0_xattn_Wk"].T),
        "wv_t": rows(got["L0_xattn_Wv"].T),
        "bq": cols(got["L0_xattn_bq"]),
        "bk": cols(got["L0_xattn_bk"]),
        "bv": np.broadcast_to(got["L0_xattn_bv"].reshape(1, E), (P, E)),
        "router": rows(got["L0_ffn_router"]),
        "w_gu": rows(gate_up),
        "w_down": rows(got["L0_ffn_experts_down"]),
        "s_gu": rows(shared_gate_up),
        "s_down": rows(got["L0_ffn_shared_down"]),
    }
    arrays = {f"in_{k}": np.ascontiguousarray(v) for k, v in arrays.items()}
    nc = bacc.Bacc("TRN2", target_bir_lowering=False, num_devices=1)
    args = [nc.dram_tensor(k, v.shape, mybir.dt.from_np(v.dtype), kind="ExternalInput").ap() for k, v in arrays.items()]
    out = nc.dram_tensor("out", (B, S, E), F32, kind="ExternalOutput").ap()
    build(nc, *args, out)
    r = run_bass_kernel_spmd(nc, [arrays], core_ids=[0])
    return r.results[0]["out"]
```
